# Optimizing a Trainium2 kernel written in Bass

```python
import numpy as np
import jax
import jax.numpy as jnp

def _softmax(x, axis=-1):
    return jax.nn.softmax(x, axis=axis)

def _gelu(x):
    return jax.nn.gelu(x, approximate=True)

def _silu(x):
    return jax.nn.silu(x)

def _sigmoid(x):
    return jax.nn.sigmoid(x)

def _layernorm(x, axis=-1, eps=1e-05):
    m = jnp.mean(x, axis=axis, keepdims=True)
    v = jnp.var(x, axis=axis, keepdims=True)
    return (x - m) / jnp.sqrt(v + eps)

def _scatter_add(tgt, idx, src, axis=0):
    return tgt.at[idx].add(src)

def _segment_sum(src, seg, n):
    return jax.ops.segment_sum(src, seg, n)
kernel_name = 'mk_prb_d1_jaxref_r4_e9536c'

def setup_inputs(seed: int=0):
    np.random.seed(seed)
    _w = jnp.asarray

    def _L0_attn_setup():
        import jax, jax.numpy as jnp
        import numpy as np
        D_MODEL = 256
        N_HEADS = 16
        D_HEAD = D_MODEL // N_HEADS
        B, T = (2, 512)
        EPS = 1e-05
        key = jax.random.key(seed)
        ks = jax.random.split(key, 5)
        s = 1.0 / np.sqrt(D_MODEL)
        return {'x': jax.random.normal(ks[0], (B, T, D_MODEL), dtype=jnp.float32), 'W_q': jax.random.normal(ks[1], (D_MODEL, D_MODEL), dtype=jnp.float32) * s, 'W_k': jax.random.normal(ks[2], (D_MODEL, D_MODEL), dtype=jnp.float32) * s, 'W_v': jax.random.normal(ks[3], (D_MODEL, D_MODEL), dtype=jnp.float32) * s, 'W_o': jax.random.normal(ks[4], (D_MODEL, D_MODEL), dtype=jnp.float32) * s, 'gn_weight': jnp.ones((D_MODEL,), dtype=jnp.float32), 'gn_bias': jnp.zeros((D_MODEL,), dtype=jnp.float32)}
    _L0_attn_in = _L0_attn_setup()

    def _L0_ffn_setup():
        import jax, jax.numpy as jnp
        import numpy as np
        D, H, O, E, TOPK = (256, 1024, 256, 8, 2)
        B, L = (2, 512)
        ROUTE_SCALE = 1.0
        key = jax.random.key(seed)
        ks = jax.random.split(key, 7)
        gb = float(np.sqrt(6.0 / (E + D)))
        return {'x': jax.random.normal(ks[0], (B, L, D), dtype=jnp.float32), 'gate_w': jax.random.uniform(ks[1], (E, D), jnp.float32, -gb, gb), 'gate_b': jnp.zeros((E,), jnp.float32), 'w1': jax.random.normal(ks[2], (E, D, H), jnp.float32) * 0.02, 'b1': jnp.zeros((E, H), jnp.float32), 'w2': jax.random.normal(ks[3], (E, H, O), jnp.float32) * 0.02, 'b2': jnp.zeros((E, O), jnp.float32)}
    _L0_ffn_in = _L0_ffn_setup()
    _d = {'L0_attn_x': _L0_attn_in['x'], 'L0_attn_W_q': _L0_attn_in['W_q'], 'L0_attn_W_k': _L0_attn_in['W_k'], 'L0_attn_W_v': _L0_attn_in['W_v'], 'L0_attn_W_o': _L0_attn_in['W_o'], 'L0_attn_gn_weight': _L0_attn_in['gn_weight'], 'L0_attn_gn_bias': _L0_attn_in['gn_bias'], 'L0_ffn_gate_w': _L0_ffn_in['gate_w'], 'L0_ffn_gate_b': _L0_ffn_in['gate_b'], 'L0_ffn_w1': _L0_ffn_in['w1'], 'L0_ffn_b1': _L0_ffn_in['b1'], 'L0_ffn_w2': _L0_ffn_in['w2'], 'L0_ffn_b2': _L0_ffn_in['b2']}
    _x0 = _d['L0_attn_x']
    _d['L0_attn_x'] = jax.random.normal(jax.random.fold_in(jax.random.key(seed), 1), (4, 1024, 256), dtype=_x0.dtype)
    del _x0
    return _d

def reference(L0_attn_x, L0_attn_W_q, L0_attn_W_k, L0_attn_W_v, L0_attn_W_o, L0_attn_gn_weight, L0_attn_gn_bias, L0_ffn_gate_w, L0_ffn_gate_b, L0_ffn_w1, L0_ffn_b1, L0_ffn_w2, L0_ffn_b2):

    def _L0_attn_ref(x, W_q, W_k, W_v, W_o, gn_weight, gn_bias):
        import jax, jax.numpy as jnp
        import numpy as np
        D_MODEL = 256
        N_HEADS = 16
        D_HEAD = D_MODEL // N_HEADS
        B, T = (2, 512)
        EPS = 1e-05
        b, t, dm = x.shape
        h, dh = (N_HEADS, D_HEAD)
        gammas = 1.0 - 2.0 ** (-5.0 - jnp.arange(h, dtype=jnp.float32))
        q = (x @ W_q.T).reshape(b, t, h, dh)
        k = (x @ W_k.T).reshape(b, t, h, dh)
        v = (x @ W_v.T).reshape(b, t, h, dh)
        idx = jnp.arange(t)
        diff = idx[:, None] - idx[None, :]
        pow_ = jnp.maximum(diff, 0).astype(jnp.float32)
        decay = jnp.where(diff >= 0, gammas[:, None, None] ** pow_, 0.0)
        scale = jnp.sqrt(jnp.float32(dh))
        attn = jnp.einsum('bihd,bjhd->bhij', q, k) * decay[None] / scale
        y = jnp.einsum('bhij,bjhd->bihd', attn, v)
        mean = y.mean(axis=(1, 3), keepdims=True)
        var = y.var(axis=(1, 3), keepdims=True)
        yn = (y - mean) / jnp.sqrt(var + EPS)
        yn = yn.reshape(b, t, dm) * gn_weight + gn_bias
        return yn @ W_o.T

    def _L0_ffn_ref(x, gate_w, gate_b, w1, b1, w2, b2):
        import jax, jax.numpy as jnp
        import numpy as np
        D, H, O, E, TOPK = (256, 1024, 256, 8, 2)
        B, L = (2, 512)
        ROUTE_SCALE = 1.0
        Bb, Ll, Dd = x.shape
        N = Bb * Ll
        x_flat = x.reshape(N, Dd)
        logits = x_flat @ gate_w.T + gate_b
        probs = jax.nn.softmax(logits * ROUTE_SCALE, axis=-1)
        topk_vals, topk_idx = jax.lax.top_k(probs, TOPK)
        dense_gate = jnp.zeros((N, E), probs.dtype).at[jnp.arange(N)[:, None], topk_idx].set(topk_vals)
        h = jax.nn.relu(jnp.einsum('nd,edh->neh', x_flat, w1) + b1)
        y = jnp.einsum('neh,eho->neo', h, w2) + b2
        out_flat = jnp.einsum('ne,neo->no', dense_gate, y)
        return out_flat.reshape(Bb, Ll, O)
    x = L0_attn_x
    xn = _layernorm(x, axis=-1)
    x = x + _L0_attn_ref(xn, L0_attn_W_q, L0_attn_W_k, L0_attn_W_v, L0_attn_W_o, L0_attn_gn_weight, L0_attn_gn_bias) + _L0_ffn_ref(xn, L0_ffn_gate_w, L0_ffn_gate_b, L0_ffn_w1, L0_ffn_b1, L0_ffn_w2, L0_ffn_b2)
    return x

_drawn_inputs = setup_inputs


def setup_inputs(seed=0):
    import zlib

    import numpy as np

    out = dict(_drawn_inputs(seed))
    spreads = {'L0_attn_gn_weight': (1.0, 0.2),
     'L0_attn_gn_bias': (0.0, 0.1),
     'L0_ffn_gate_b': (0.0, 0.721),
     'L0_ffn_b1': (0.0, 0.474),
     'L0_ffn_b2': (0.0, 0.1)}
    factors = {}
    for name, (base, spread) in spreads.items():
        noise = np.random.default_rng([zlib.crc32(name.encode()), seed]).standard_normal(out[name].shape)
        drawn = base * np.exp(spread * noise) if base else spread * noise
        out[name] = jnp.asarray(drawn.astype(out[name].dtype))
    for name, factor in factors.items():
        out[name] = (out[name] * factor).astype(out[name].dtype)
    return out
```

```python
from contextlib import ExitStack

import numpy as np

import concourse.bass as bass
from concourse import mybir

F32 = mybir.dt.float32
FR = mybir.dt.float32r
BF16 = mybir.dt.bfloat16
I32 = mybir.dt.int32
ALU = mybir.AluOpType
ACT = mybir.ActivationFunctionType
AX = mybir.AxisListType.X

P = 128
B, T, D = 4, 1024, 256
KC = D // P
NT = B * T // P
CB = T // P
H, DH = 16, 16
HP = P // DH
RG = 4
E, F = 8, 1024
FC = F // P
SLOT = 512
SJ = SLOT // P
NS = (2 * NT * P - E) // SLOT + E
NK = NT * P // SLOT
EPS = 1e-5
GRP = 4
NG = NT // GRP
BIG = 1e30

PASSES = ((0, 0), (0, 1), (1, 0))


def constants():
    i = np.arange(P)
    gam = 1.0 - 2.0 ** (-5.0 - np.arange(H, dtype=np.float64))
    head = (np.arange(D) // DH)
    local = (i % P) // DH
    tab_q = np.stack([gam[c * HP + local][:, None] ** (i[None, :] - 64) for c in range(KC)], 1) / np.sqrt(DH)
    same = local[:, None] == local[None, :]
    decay = np.stack([same * (gam[c * HP + local] ** P)[:, None] for c in range(KC)], 1)
    keep = np.ones((P, NT + 1))
    keep[:, ::CB] = 0.0
    cols = {
        "ident": np.eye(P),
        "causal": (i[None, :] >= i[:, None]) * 1.0,
        "tab_q": tab_q.reshape(P, -1),
        "tab_k": gam[head][None, :] ** (64.0 - i[:, None]),
        "decay": decay.reshape(P, -1),
        "group_mean": same / DH,
        "parity": np.stack([local % 2 == 0, local % 2 == 1], 1) * 1.0,
        "keep": keep,
        "slot_rows": np.tile(np.arange(NK) * float(SLOT), (P, 1)),
        "slot_no": np.tile(np.arange(NS) * 1.0, (P, 1)),
        "expert_no": np.tile(np.arange(E) * 1.0, (P, 1)),
        "rank_low": np.tile(E - np.arange(E) * 1.0, (P, 1)),
    }
    at, where = 0, {}
    for name, a in cols.items():
        where[name] = (at, at + a.shape[1])
        at += a.shape[1]
    return np.concatenate(list(cols.values()), 1).astype(np.float32), where


def run_steps(eng, first, last, lo, hi, step):
    for i in range(first, lo):
        step(i, i % 2)
    assert lo % 2 == 0 and hi % 2 == 0
    with eng.Fori(lo // 2, hi // 2) as pair:
        step(pair * 2, 0)
        step(pair * 2 + 1, 1)
    for i in range(hi, last):
        step(i, i % 2)


def run_batches(eng, count, batch):
    batch(0)
    with eng.Fori(1, count) as b:
        batch(b)


def within(n, count):
    return not isinstance(n, int) or 0 <= n < count


def wait(eng, sem, value):
    if isinstance(value, int) and value <= 0:
        return
    eng.wait_ge(sem, value)


def build(nc, where, x, wq_t, wkv_t, wo_t, gn, gate_t, gate_b, w1, w2, b1_t, b2, const, out):
    xs_rows = nc.dram_tensor("xs_rows", [NS * SLOT, D], F32).ap()
    ys_rows = nc.dram_tensor("ys_rows", [NS * SLOT, D], F32).ap()
    x_tiles = x.rearrange("b (c p) d -> p (b c) d", p=P)
    out_tiles = out.rearrange("b (c p) d -> p (b c) d", p=P)
    xs_slots = xs_rows.rearrange("(s p j) d -> s p (j d)", p=P, j=SJ)
    ys_slots = ys_rows.rearrange("(s p j) d -> s p (j d)", p=P, j=SJ)

    with ExitStack() as ctx:
        def sb(name, shape, dt=F32):
            return ctx.enter_context(nc.sbuf_tensor(name, shape, dt))

        def sem(name):
            return ctx.enter_context(nc.semaphore(name))

        class Arena:

            def __init__(self, name, words, dt):
                self.t, self.words, self.at = sb(name, [P, words], dt), words, 0

            def __call__(self, *dims):
                n = int(np.prod(dims))
                a = self.t[:, self.at:self.at + n]
                self.at += n
                assert self.at <= self.words, (self.at, self.words)
                names = "abcd"[:len(dims)]
                if len(dims) > 1:
                    a = a.rearrange(f"p ({' '.join(names)}) -> p {' '.join(names)}",
                                    **{k: v for k, v in zip(names, dims)})
                return a

        cst = sb("cst", [P, const.shape[1]])
        C = {k: cst[:, a:b] for k, (a, b) in where.items()}
        ident = C["ident"]
        tab_q = C["tab_q"].rearrange("p (c i) -> p c i", c=KC)
        decay = C["decay"].rearrange("p (c i) -> p c i", c=KC)
        xn = sb("xn", [P, NT, D])
        part_out = xn
        wq = sb("wq", [P, 2, KC, D], FR)
        wkv = sb("wkv", [P, 2, KC, 2 * D], FR)
        wo = sb("wo", [P, 2, KC, D], FR)
        gn_sb = sb("gn_sb", [P, 2, KC])
        gate_w = sb("gate_w", [P, KC, E])
        gate_bias = sb("gate_bias", [P, E])
        b1_sb = sb("b1_sb", [P, FC, E])
        b2_sb = sb("b2_sb", [E, D])
        gates = sb("gates", [P, NT, E])
        gate2 = sb("gate2", [P, NT, 2])
        rows2 = sb("rows2", [P, NT, 2], I32)
        b1_slot = sb("b1_slot", [P, NS, FC])
        expert_of = sb("expert_of", [P, NS], I32)
        logits = sb("logits", [P, NT, E])
        ident_bf = sb("ident_bf", [P, 2, P], BF16)
        mask_bf = sb("mask_bf", [P, NT * E], BF16)
        eps_col = sb("eps_col", [P, 1])
        fence_d = sb("fence_d", [P, 1])
        fence_p = sb("fence_p", [P, 1])
        zero_rows = sb("zero_rows", [P, SJ * D // 2])

        fr = Arena("arena_r", 18432, FR)
        ff = Arena("arena_f", 13312, F32)

        w_raw = ff(2 * D * KC)
        x_raw = ff(2, GRP, D)
        x_grp = ff(2, GRP, D)
        x_grp_t = ff(2, KC, GRP * P)
        stats = sb("stats", [P, 2, GRP, 6])
        mean_var = sb("mean_var", [P, 2, GRP, 2])
        std = sb("std", [P, 2, GRP])
        rstd = sb("rstd", [P, 2, GRP])
        ff.at = w_raw.shape[1]
        rt = [ff(NT, E) for _ in range(6)]
        rs = sb("rs", [P, 12, NT])
        re = sb("re", [P, 12, E])
        rk = sb("rk", [P, E, NK])
        rsl = ff(NS, FC, E)
        rse = ff(NS, E)
        ff.at = 0
        y_t = ff(KC, NT * P)
        x_chunk = [sb(f"x_chunk{i}", [P, D]) for i in range(2)]
        row_chunk = [sb(f"row_chunk{i}", [P, 2], I32) for i in range(2)]
        k_f = ff(2, D)
        q_f = ff(2, KC, P)
        s_f = ff(2, 4 * P)
        y_f = ff(2, D)
        state_f = ff(KC, P)
        state_t = ff(KC, P)
        xt = fr(2, 2, KC * P)
        k_r = fr(2, 2, D)
        v_r = fr(2, 2, D)
        q_r = fr(2, 2, KC * P)
        keo = fr(2, 4, KC * P)
        s_r = fr(4, RG, 4 * P)
        state_r = fr(2, KC * P)
        yn_f = ff(KC, 4 * P)
        x_res = ff(4, D)
        yn_r = fr(2, KC, 4 * P)
        bstat = sb("bstat", [P, KC, 2, 6])
        bmv = sb("bmv", [P, KC, 2])
        bsm = sb("bsm", [P, 8, KC])
        gate_b4 = sb("gate_b4", [P, 4, E])
        gate_t4 = sb("gate_t4", [E, 4, P])
        ff.at = fr.at = 0
        w1_raw = ff(KC * F)
        w2_raw = ff(FC * D)
        xs = ff(2, SJ, D)
        h_f = ff(2, SLOT)
        ys = ff(SJ * D)
        w1_r = fr(2, KC, F)
        w2_r = fr(2, FC, D)
        h_r = fr(2, FC, SLOT)
        xs_r = fr(2, KC * SLOT)
        ff.at = 0
        y_pair = [ff(2, D) for _ in range(4)]
        out_sb = ff(4, D)

        ps = ctx.enter_context(nc.psum_tensor("ps", [P, 8, 512], F32))

        s = {}
        for name in (
            "consts_in weights_in gn_in small_in w_raw_free w_split_h w_split_l zeroed rows_zero "
            "x_in0 x_in1 ln_stats ln_var ln_std ln_rstd ln_xg ln_t_psum ln_t_sb ln_logit_psum ln_logit ln_xn "
            "route dve_route route_exp route_mask route_psum route_done b1_done tri_done "
            "xc rc xt_psum xt_h xt_l kv_psum q_psum k_f k_h k_l v_h v_l q_f q_h q_l kt_psum keo_h keo_l "
            "s_psum s_f s_h s_l y_psum across_done u_psum st_t st_f st_h st_l y_f yt_psum y_t scat0 scat1 st_zero "
            "gn_chain gn_mv gn_avg_psum gn_std gn_ab yn_f yn_h yn_l g4 g4_psum g4_sb o_psum o_done x_res_in "
            "w1_in w2_in xs_in0 xs_in1 w1_h w1_l w2_h w2_l xst_psum xst_h xst_l h_psum h_f h_h h_l l1_done "
            "ys_psum ys_sb ys_out pair0 pair1 pair2 pair3 f_x f_a f_b out_done"
        ).split():
            s[name] = sem(name)

        block = ctx.enter_context(nc.Block())

        @block.sync
        def _(sp):
            sp.dma_start(cst[:], const).then_inc(s["consts_in"], 16)

            def ln_load(g, par):
                wait(sp, s["ln_xg"], g - 1)
                sp.dma_start(x_raw[:, par], x_tiles[:, bass.ds(g * GRP, GRP), :]).then_inc(s[f"x_in{par}"], 16)

            ln_load(0, 0)
            ln_load(1, 1)
            sp.dma_start(gate_w[:], gate_t.rearrange("(k p) e -> p k e", p=P)).then_inc(s["small_in"], 16)
            sp.dma_start(gate_bias[:], gate_b.rearrange("(a e) -> a e", a=1).to_broadcast([P, E])).then_inc(s["small_in"], 16)
            sp.dma_start(b1_sb[:], b1_t).then_inc(s["small_in"], 16)
            sp.dma_start(b2_sb[:], b2).then_inc(s["small_in"], 16)
            sp.dma_start(gn_sb[:], gn).then_inc(s["small_in"], 16)
            run_steps(sp, 2, NG, 2, NG, ln_load)
            for n, (src, cols) in enumerate(((wq_t, D), (wkv_t, 2 * D), (wo_t, D))):
                if n:
                    sp.wait_ge(s["w_split_h"], n)
                    sp.wait_ge(s["w_split_l"], n)
                sp.dma_start(w_raw[:, 0:KC * cols].rearrange("p (k n) -> p k n", k=KC),
                             src.rearrange("(k p) n -> p k n", p=P)).then_inc(s["weights_in"], 16)
            sp.wait_ge(s["zeroed"], 1)
            with sp.Fori(0, NS) as sl:
                for half in range(2):
                    w = SJ * D // 2
                    sp.dma_start(xs_slots[bass.ds(sl, 1), :, half * w:half * w + w].rearrange("a p d -> (a p) d"),
                                 zero_rows[:]).then_inc(s["rows_zero"], 16)
            def residual_load(hb):
                wait(sp, s["o_done"], hb * 4)
                sp.dma_start(x_res, x_tiles[:, bass.ds(hb * 4, 4), :]).then_inc(s["x_res_in"], 16)

            run_batches(sp, 2 * B, residual_load)
            sp.wait_ge(s["route_done"], 1)
            for par in range(2):
                sp.wait_ge(s[f"scat{par}"], 16 * NT)
            sp.wait_ge(s["o_done"], NT)
            sp.wait_ge(s["b1_done"], 1)

            def slot_load(sl, par):
                e = sp.value_load(expert_of[0:1, bass.ds(sl, 1)], min_val=0, max_val=E - 1)
                wait(sp, s["xst_psum"], sl - 1)
                sp.dma_start(xs[:, par].rearrange("p j d -> p (j d)"),
                             xs_slots[bass.ds(sl, 1)].rearrange("a p d -> (a p) d")).then_inc(s[f"xs_in{par}"], 16)
                wait(sp, s["w1_h"], sl)
                wait(sp, s["w1_l"], sl)
                sp.dma_start(w1_raw, w1[bass.ds(e, 1)].rearrange("a p n -> (a p) n")).then_inc(s["w1_in"], 16)
                wait(sp, s["w2_h"], sl)
                wait(sp, s["w2_l"], sl)
                sp.dma_start(w2_raw, w2[bass.ds(e, 1)].rearrange("a p n -> (a p) n")).then_inc(s["w2_in"], 16)

            def slot_store(sl):
                sp.wait_ge(s["ys_sb"], sl + 1)
                sp.dma_start(ys_slots[bass.ds(sl, 1)].rearrange("a p d -> (a p) d"), ys).then_inc(s["ys_out"], 16)

            slot_load(0, 0)

            def slot_step(sl, par):
                if within(sl - 1, NS):
                    slot_store(sl - 1)
                if within(sl + 1, NS):
                    slot_load(sl + 1, 1 - par)

            run_steps(sp, 0, NS + 1, 2, NS - 1, slot_step)
            def out_store(t4):
                sp.wait_ge(s["f_b"], 4 * t4 + 4)
                sp.dma_start(out_tiles[:, bass.ds(t4 * 4, 4), :], out_sb).then_inc(s["out_done"], 16)

            run_batches(sp, NT // 4, out_store)
            sp.wait_ge(s["out_done"], 16 * (NT // 4))
            sp.wait_ge(s["ys_out"], 16 * NS)
            sp.wait_ge(s["rows_zero"], 32 * NS)

        @block.gpsimd
        def _(pool):
            nc.gpsimd.memset(zero_rows[:], 0.0).then_inc(s["zeroed"], 1)
            pool.wait_ge(s["zeroed"], 1)
            nc.gpsimd.memset(state_r.bitcast(F32), 0.0).then_inc(s["st_zero"], 1)
            for n, (dst, cols) in enumerate(((wq, D), (wkv, 2 * D), (wo, D))):
                pool.wait_ge(s["weights_in"], 16 * (n + 1))
                pool.wait_ge(s["w_split_h"], n + 1)
                raw = w_raw[:, 0:KC * cols]
                flat = dst[:].rearrange("p s k n -> p s (k n)")
                nc.gpsimd.tensor_tensor(flat[:, 1], raw, flat[:, 0].bitcast(F32), ALU.subtract).then_inc(s["w_split_l"], 1)
            pool.wait_ge(s["rows_zero"], 32 * NS)
            pool.wait_ge(s["ln_xn"], NG)
            pool.wait_ge(s["route_done"], 1)

            def chunk_copy(n, par):
                wait(pool, s["xt_psum"], n - 1)
                wait(pool, s[f"scat{par}"], (n - par) * 16)
                nc.gpsimd.tensor_copy(x_chunk[par][:], xn[:, bass.ds(n, 1), :].rearrange("p a d -> p (a d)")).then_inc(s["xc"], 1)
                nc.gpsimd.tensor_copy(row_chunk[par][:], rows2[:, bass.ds(n, 1), :].rearrange("p a d -> p (a d)")).then_inc(s["rc"], 1)

            def chunk_scatter(n, par):
                pool.wait_ge(s["xc"], n + 1)
                pool.wait_ge(s["rc"], n + 1)
                nc.gpsimd.tensor_tensor(fence_p[:, 0:1], zero_rows[:, 0:1], zero_rows[:, 0:1], ALU.add)
                for k in range(2):
                    nc.gpsimd.indirect_dma_start(
                        xs_rows, bass.IndirectOffsetOnAxis(ap=row_chunk[par][:, k:k + 1], axis=0),
                        x_chunk[par][:], None).then_inc(s[f"scat{par}"], 16)

            def step(i, par):
                if within(i, NT):
                    for g in range(RG):
                        pool.wait_ge(s["s_h"], RG * i + g + 1)
                        wait(pool, s["y_psum"], i - 1)
                        nc.gpsimd.tensor_tensor(s_r[:, 2 * par + 1, g], s_f[:, g % 2],
                                                s_r[:, 2 * par, g].bitcast(F32), ALU.subtract).then_inc(s["s_l"], 1)
                n, np_ = i + 1, 1 - par
                if within(n, NT):
                    pool.wait_ge(s["k_h"], n + 1)
                    nc.gpsimd.tensor_tensor(k_r[:, np_, 1], k_f[:, np_], k_r[:, np_, 0].bitcast(F32), ALU.subtract).then_inc(s["k_l"], 1)
                    pool.wait_ge(s["q_h"], n + 1)
                    nc.gpsimd.tensor_tensor(q_r[:, np_, 1], q_f[:, np_].rearrange("p c i -> p (c i)"),
                                            q_r[:, np_, 0].bitcast(F32), ALU.subtract).then_inc(s["q_l"], 1)
                if within(i - 1, NT):
                    pool.wait_ge(s["st_h"], i)
                    nc.gpsimd.tensor_tensor(state_r[:, 1], state_f.rearrange("p c i -> p (c i)"),
                                            state_r[:, 0].bitcast(F32), ALU.subtract).then_inc(s["st_l"], 1)
                if within(i + 3, NT):
                    chunk_copy(i + 3, 1 - par)
                    chunk_scatter(i + 3, 1 - par)

            chunk_copy(0, 0)
            chunk_scatter(0, 0)
            run_steps(pool, -2, NT + 1, 4, 28, step)

            def slot_step(sl, par):
                pool.wait_ge(s["w2_h"], sl + 1)
                nc.gpsimd.tensor_tensor(w2_r[:, 1].rearrange("p k n -> p (k n)"), w2_raw,
                                        w2_r[:, 0].rearrange("p k n -> p (k n)").bitcast(F32), ALU.subtract).then_inc(s["w2_l"], 1)
                if within(sl + 1, NS):
                    w1_low(sl + 1)

            def w1_low(sl):
                pool.wait_ge(s["w1_h"], sl + 1)
                nc.gpsimd.tensor_tensor(w1_r[:, 1].rearrange("p k n -> p (k n)"), w1_raw,
                                        w1_r[:, 0].rearrange("p k n -> p (k n)").bitcast(F32), ALU.subtract).then_inc(s["w1_l"], 1)

            w1_low(0)
            run_steps(pool, 0, NS, 0, NS - 1, slot_step)
            pool.wait_ge(s["ys_out"], 16 * NS)
            pool.wait_ge(s["h_l"], NS * FC)
            for t in range(NT):
                b4 = t % 4
                wait(pool, s["f_b"], t - 3)
                for k in range(2):
                    nc.gpsimd.indirect_dma_start(
                        y_pair[b4][:, k, :], None, ys_rows,
                        bass.IndirectOffsetOnAxis(ap=rows2[:, t, k:k + 1], axis=0)).then_inc(s[f"pair{b4}"], 16)

        @block.scalar
        def _(act):
            def ln_std(g, par):
                act.wait_ge(s["ln_var"], g + 1)
                nc.scalar.activation(std[:, par], mean_var[:, par, :, 1], ACT.Sqrt, bias=eps_col[:, 0:1]).then_inc(s["ln_std"], 1)

            def ln_copies(g, par):
                act.wait_ge(s["ln_xg"], g + 1)
                nc.scalar.activation(xn[:, bass.ds(g * GRP, GRP), :], x_grp[:, par], ACT.Copy).then_inc(s["ln_xn"], 1)
                wait(act, s["ln_logit_psum"], g - 1)
                for k in range(KC):
                    act.wait_ge(s["ln_t_psum"], KC * g + k + 1)
                    nc.scalar.activation(x_grp_t[:, par, k], ps[:, 2 * par + k, :], ACT.Copy).then_inc(s["ln_t_sb"], 1)

            def step(g, par):
                if within(g + 1, NG):
                    ln_std(g + 1, 1 - par)
                if within(g, NG):
                    ln_copies(g, par)

            act.wait_ge(s["tri_done"], 3)
            run_steps(act, -1, NG, 2, NG - 2, step)
            for n, (dst, cols) in enumerate(((wq, D), (wkv, 2 * D), (wo, D))):
                act.wait_ge(s["weights_in"], 16 * (n + 1))
                nc.scalar.activation(dst[:].rearrange("p s k n -> p s (k n)")[:, 0], w_raw[:, 0:KC * cols], ACT.Copy).then_inc(s["w_split_h"], 1)
            act.wait_ge(s["route"], 1)
            nc.scalar.activation(rt[2], rt[1], ACT.Exp).then_inc(s["route_exp"], 1)

            def chunk(i, par):
                if within(i, NT):
                    for g in range(RG):
                        act.wait_ge(s["s_f"], RG * i + g + 1)
                        wait(act, s["y_psum"], i - 1)
                        nc.scalar.activation(s_r[:, 2 * par, g], s_f[:, g % 2], ACT.Copy).then_inc(s["s_h"], 1)
                n, np_ = i + 1, 1 - par
                if within(n, NT):
                    wait(act, s["y_psum"], n - 1)
                    act.wait_ge(s["k_f"], n + 1)
                    nc.scalar.activation(v_r[:, np_, 0], ps[:, 4, D:2 * D], ACT.Copy).then_inc(s["v_h"], 1)
                    nc.scalar.activation(k_r[:, np_, 0], k_f[:, np_], ACT.Copy).then_inc(s["k_h"], 1)
                    act.wait_ge(s["q_f"], n + 1)
                    nc.scalar.activation(q_r[:, np_, 0], q_f[:, np_].rearrange("p c i -> p (c i)"), ACT.Copy).then_inc(s["q_h"], 1)
                if within(i - 1, NT):
                    act.wait_ge(s["st_f"], i)
                    act.wait_ge(s["across_done"], i)
                    nc.scalar.activation(state_r[:, 0], state_f.rearrange("p c i -> p (c i)"), ACT.Copy).then_inc(s["st_h"], 1)
                if within(n, NT):
                    act.wait_ge(s["kt_psum"], n + 1)
                    wait(act, s["s_psum"], RG * (n - 1))
                    for odd in range(2):
                        nc.scalar.activation(keo[:, np_, odd], ps[:, 5, 0:256], ACT.Copy,
                                             scale=C["parity"][:, odd:odd + 1]).then_inc(s["keo_h"], 1)
                if within(i - 1, NT):
                    m = i - 1
                    act.wait_ge(s["y_psum"], m + 1)
                    wait(act, s["yt_psum"], m - 1)
                    nc.scalar.activation(y_f[:, 1 - par], ps[:, 7, 0:D], ACT.Copy).then_inc(s["y_f"], 1)
                if within(i - 2, NT):
                    m = i - 2
                    act.wait_ge(s["yt_psum"], m + 1)
                    nc.scalar.activation(y_t[:, :, bass.ds(m * P, P)], ps[:, 6, 0:256].rearrange("p (c i) -> p c i", c=KC),
                                         ACT.Copy).then_inc(s["y_t"], 1)
                if within(i + 2, NT):
                    m = i + 2
                    act.wait_ge(s["xt_psum"], m + 1)
                    wait(act, s["q_psum"], m - 1)
                    nc.scalar.activation(xt[:, par, 0], ps[:, 4, 0:256], ACT.Copy).then_inc(s["xt_h"], 1)

            run_steps(act, -2, NT + 2, 4, 28, chunk)

            def norm_batch(b):
                act.wait_ge(s["gn_mv"], b + 1)
                nc.scalar.activation(bsm[:, 3], bsm[:, 2], ACT.Sqrt, bias=eps_col[:, 0:1]).then_inc(s["gn_std"], 1)
                act.wait_ge(s["gn_ab"], b + 1)
                for half in range(2):
                    hb = b * 2 + half
                    for c in range(KC):
                        wait(act, s["yn_l"], hb)
                        nc.scalar.activation(yn_f[:, c], y_t[:, c, bass.ds(hb * 512, 512)], ACT.Identity,
                                             scale=bsm[:, 5, c:c + 1], bias=bsm[:, 6, c:c + 1]).then_inc(s["yn_f"], 1)
                    act.wait_ge(s["yn_f"], hb * 2 + 2)
                    wait(act, s["o_psum"], hb * 4)
                    nc.scalar.activation(yn_r[:, 0], yn_f, ACT.Copy).then_inc(s["yn_h"], 1)
                    act.wait_ge(s["g4_psum"], hb + 1)
                    nc.scalar.activation(gate_t4[:].rearrange("e t i -> e (t i)"), ps[0:E, 4, :], ACT.Copy).then_inc(s["g4_sb"], 1)

            run_batches(act, B, norm_batch)

            def w1_high(sl):
                act.wait_ge(s["w1_in"], 16 * (sl + 1))
                wait(act, s["h_psum"], FC * sl)
                nc.scalar.activation(w1_r[:, 0].rearrange("p k n -> p (k n)"), w1_raw, ACT.Copy).then_inc(s["w1_h"], 1)

            def xs_high(sl):
                act.wait_ge(s["xst_psum"], sl + 1)
                wait(act, s["h_psum"], FC * sl)
                nc.scalar.activation(xs_r[:, 0].rearrange("p (k n) -> p k n", k=KC), ps[:, 0:2, :], ACT.Copy).then_inc(s["xst_h"], 1)

            def slot_step(sl, par):
                for hc in range(FC):
                    m = sl * FC + hc
                    act.wait_ge(s["h_psum"], m + 1)
                    wait(act, s["h_l"], m - 1)
                    nc.scalar.activation(h_f[:, hc % 2], ps[:, 2 + hc % 4, :], ACT.Relu,
                                         bias=b1_slot[:, bass.ds(sl, 1), hc:hc + 1].rearrange("p a b -> p (a b)")).then_inc(s["h_f"], 1)
                    if hc == 1:
                        act.wait_ge(s["w2_in"], 16 * (sl + 1))
                        wait(act, s["ys_psum"], sl)
                        nc.scalar.activation(w2_r[:, 0].rearrange("p k n -> p (k n)"), w2_raw, ACT.Copy).then_inc(s["w2_h"], 1)
                if within(sl + 1, NS):
                    xs_high(sl + 1)
                    w1_high(sl + 1)

            w1_high(0)
            xs_high(0)
            run_steps(act, 0, NS, 2, NS - 1, slot_step)

        @block.tensor
        def _(pe):
            pe.wait_ge(s["consts_in"], 16)
            pe.wait_ge(s["small_in"], 80)

            def parts(out_ap, lhs, rhs, start, stop, **kw):
                for n, (a, b) in enumerate(PASSES):
                    last = pe.matmul(out_ap, lhs(a), rhs(b), start=start and n == 0, stop=stop and n == 2, **kw)
                return last

            def ln_transposes(g, par):
                pe.wait_ge(s["ln_xg"], g + 1)
                wait(pe, s["ln_t_sb"], KC * (g - 1))
                for k in range(KC):
                    for t in range(GRP):
                        last = pe.transpose(ps[:, 2 * par + k, t * P:(t + 1) * P], x_grp[:, par, t, k * P:(k + 1) * P], ident)
                    last.then_inc(s["ln_t_psum"], 1)

            def ln_logits(g, par):
                pe.wait_ge(s["ln_t_sb"], KC * (g + 1))
                wait(pe, s["ln_logit"], g - 1)
                for t in range(GRP):
                    for k in range(KC):
                        last = pe.matmul(ps[:, 4 + par, t * E:(t + 1) * E], x_grp_t[:, par, k, t * P:(t + 1) * P], gate_w[:, k, :],
                                         start=(k == 0), stop=(k == KC - 1))
                last.then_inc(s["ln_logit_psum"], 1)

            def ln_step(g, par):
                if within(g, NG):
                    ln_transposes(g, par)
                if within(g - 1, NG):
                    ln_logits(g - 1, 1 - par)

            run_steps(pe, 0, NG + 1, 4, NG, ln_step)

            pe.wait_ge(s["route_mask"], 1)
            pe.wait_ge(s["tri_done"], 3)
            for k in range(2):
                last = pe.matmul(ps[:, 6 + k, 0:NT * E], ident_bf[:, k], mask_bf[:], start=True, stop=True)
            last.then_inc(s["route_psum"], 1)
            pe.wait_ge(s["w_split_h"], 3)
            pe.wait_ge(s["w_split_l"], 3)
            pe.wait_ge(s["route_done"], 1)
            pe.wait_ge(s["st_zero"], 2)

            def x_transposes(n, par):
                pe.wait_ge(s["xc"], n + 1)
                wait(pe, s["k_f"], n)
                wait(pe, s["v_l"], n)
                for k in range(KC):
                    last = pe.transpose(ps[:, 4, k * P:(k + 1) * P], x_chunk[par][:, k * P:(k + 1) * P], ident)
                last.then_inc(s["xt_psum"], 1)

            def projections(n, par):
                pe.wait_ge(s["xt_h"], n + 1)
                pe.wait_ge(s["xt_l"], n + 1)
                for m, (a, b) in enumerate(PASSES):
                    for k in range(KC):
                        last = pe.matmul(ps[:, 4, :], xt[:, par, a, k * P:(k + 1) * P], wkv[:, b, k, :],
                                         start=(m == 0 and k == 0), stop=(m == 2 and k == KC - 1))
                last.then_inc(s["kv_psum"], 1)
                wait(pe, s["keo_h"], 2 * n)
                wait(pe, s["keo_l"], 2 * n)
                for c in range(KC):
                    for m, (a, b) in enumerate(PASSES):
                        for k in range(KC):
                            last = pe.matmul(ps[:, 5, c * P:(c + 1) * P], wq[:, a, k, c * P:(c + 1) * P], xt[:, par, b, k * P:(k + 1) * P],
                                             start=(m == 0 and k == 0), stop=(m == 2 and k == KC - 1))
                last.then_inc(s["q_psum"], 1)

            def k_transposes(n, par):
                pe.wait_ge(s["k_f"], n + 1)
                pe.wait_ge(s["q_f"], n + 1)
                for c in range(KC):
                    last = pe.transpose(ps[:, 5, c * P:(c + 1) * P], k_f[:, par, c * P:(c + 1) * P], ident)
                last.then_inc(s["kt_psum"], 1)

            def scores(n, par):
                pe.wait_ge(s["keo_l"], 2 * (n + 1))
                pe.wait_ge(s["keo_h"], 2 * (n + 1))
                pe.wait_ge(s["q_h"], n + 1)
                pe.wait_ge(s["q_l"], n + 1)
                for pair in range(RG // 2):
                    groups = (2 * pair, 2 * pair + 1)
                    wait(pe, s["s_f"], RG * (n - 1) + groups[1] + 1 if not isinstance(n, int) or n > 0 else 0)
                    for c in range(KC):
                        for odd in range(2):
                            col = (2 * c + odd) * P
                            for m, (a, b) in enumerate(PASSES):
                                for g in groups:
                                    r = slice(32 * g, 32 * g + 32)
                                    last = pe.matmul(ps[:, g, col:col + P], keo[r, par, 2 * a + odd, c * P:(c + 1) * P],
                                                     q_r[r, par, b, c * P:(c + 1) * P], start=(m == 0), stop=(m == 2))
                    last.then_inc(s["s_psum"], 2)

            def across(n, par):
                wait(pe, s["st_h"], n)
                wait(pe, s["st_l"], n)
                wait(pe, s["y_f"], n)
                for c in range(KC):
                    last = parts(ps[:, 7, c * P:(c + 1) * P], lambda a: q_r[:, par, a, c * P:(c + 1) * P],
                          lambda b: state_r[:, b, c * P:(c + 1) * P], c == 0, False, skip_group_check=True)
                last.then_inc(s["across_done"], 1)

            def inside(n, par):
                pe.wait_ge(s["s_l"], RG * (n + 1))
                pe.wait_ge(s["s_h"], RG * (n + 1))
                for c in range(KC):
                    for odd in range(2):
                        for g in range(RG):
                            h = c * HP + 2 * g + odd
                            last = parts(ps[:, 7, h * DH:(h + 1) * DH],
                                         lambda a: s_r[:, 2 * par + a, g, (2 * c + odd) * P:(2 * c + odd + 1) * P],
                                         lambda b: v_r[:, par, b, h * DH:(h + 1) * DH], False,
                                         h == H - 1, skip_group_check=True)
                last.then_inc(s["y_psum"], 1)

            def state_sums(n, par):
                pe.wait_ge(s["k_h"], n + 1)
                pe.wait_ge(s["k_l"], n + 1)
                pe.wait_ge(s["v_h"], n + 1)
                pe.wait_ge(s["v_l"], n + 1)
                wait(pe, s["y_t"], n - 1)
                for c in range(KC):
                    last = parts(ps[:, 6, 256 + c * P:256 + (c + 1) * P], lambda a: k_r[:, par, a, c * P:(c + 1) * P],
                                 lambda b: v_r[:, par, b, c * P:(c + 1) * P], c == 0, c == KC - 1, skip_group_check=True)
                last.then_inc(s["u_psum"], 1)

            def y_transposes(n, par):
                pe.wait_ge(s["y_f"], n + 1)
                wait(pe, s["y_t"], n)
                pe.wait_ge(s["st_t"], min(n + 2, NT) if isinstance(n, int) else n + 2)
                for c in range(KC):
                    last = pe.transpose(ps[:, 6, c * P:(c + 1) * P], y_f[:, par, c * P:(c + 1) * P], ident)
                last.then_inc(s["yt_psum"], 1)

            def chunk(i, par):
                if within(i, NT):
                    scores(i, par)
                if within(i + 1, NT):
                    projections(i + 1, 1 - par)
                if within(i - 1, NT):
                    state_sums(i - 1, 1 - par)
                if within(i + 1, NT):
                    k_transposes(i + 1, 1 - par)
                if within(i - 1, NT):
                    across(i - 1, 1 - par)
                    inside(i - 1, 1 - par)
                if within(i - 2, NT):
                    y_transposes(i - 2, par)
                if within(i + 2, NT):
                    x_transposes(i + 2, par)

            run_steps(pe, -2, NT + 2, 4, 28, chunk)

            def out_batch(b):
                pe.wait_ge(s["gn_chain"], b * 7 + 5)
                pe.matmul(ps[:, 5, 0:2 * KC], C["group_mean"], bsm[:, 0:2].rearrange("p a c -> p (a c)"),
                          start=True, stop=True).then_inc(s["gn_avg_psum"], 1)
                for half in range(2):
                    hb = b * 2 + half
                    pe.wait_ge(s["g4"], hb + 1)
                    wait(pe, s["g4_sb"], hb)
                    for t in range(4):
                        last = pe.transpose(ps[0:E, 4, t * P:(t + 1) * P], gate_b4[:, t, :], ident)
                    last.then_inc(s["g4_psum"], 1)
                    pe.wait_ge(s["yn_h"], hb + 1)
                    pe.wait_ge(s["yn_l"], hb + 1)
                    pe.wait_ge(s["g4_sb"], hb + 1)
                    for t in range(4):
                        wait(pe, s["o_done"], hb * 4)
                        for m, (a, bb) in enumerate(PASSES):
                            for k in range(KC):
                                pe.matmul(ps[:, t, 0:D], yn_r[:, a, k, t * P:(t + 1) * P], wo[:, bb, k, :],
                                          start=(m == 0 and k == 0), stop=False)
                        pe.matmul(ps[:, t, 0:D], gate_t4[:, t, :], b2_sb[:], start=False, stop=True).then_inc(s["o_psum"], 1)

            run_batches(pe, B, out_batch)

            def slot_transposes(sl, par):
                pe.wait_ge(s[f"xs_in{par}"], (sl - par) * 8 + 16)
                wait(pe, s["xst_h"], sl)
                wait(pe, s["xst_l"], sl)
                for k in range(KC):
                    for j in range(SJ):
                        last = pe.transpose(ps[:, k, j * P:(j + 1) * P], xs[:, par, j, k * P:(k + 1) * P], ident)
                last.then_inc(s["xst_psum"], 1)

            def layer1(sl):
                pe.wait_ge(s["w1_h"], sl + 1)
                pe.wait_ge(s["w1_l"], sl + 1)
                pe.wait_ge(s["xst_h"], sl + 1)
                pe.wait_ge(s["xst_l"], sl + 1)
                for hc in range(FC):
                    if hc >= 4:
                        pe.wait_ge(s["h_f"], sl * FC + hc - 3)
                    else:
                        wait(pe, s["h_f"], (sl - 1) * FC + hc + 5 if not isinstance(sl, int) or sl else 0)
                    for m, (a, b) in enumerate(PASSES):
                        for k in range(KC):
                            last = pe.matmul(ps[:, 2 + hc % 4, :], w1_r[:, a, k, hc * P:(hc + 1) * P],
                                             xs_r[:, b, k * SLOT:(k + 1) * SLOT],
                                             start=(m == 0 and k == 0), stop=(m == 2 and k == KC - 1))
                    last.then_inc(s["h_psum"], 1)

            def layer2(sl):
                pe.wait_ge(s["w2_h"], sl + 1)
                pe.wait_ge(s["w2_l"], sl + 1)
                wait(pe, s["ys_sb"], sl)
                for hc in range(FC):
                    pe.wait_ge(s["h_l"], sl * FC + hc + 1)
                    pe.wait_ge(s["h_h"], sl * FC + hc + 1)
                    for j in range(SJ):
                        last = parts(ps[:, 6 + j // 2, (j % 2) * D:(j % 2 + 1) * D], lambda a: h_r[:, a, hc, j * P:(j + 1) * P],
                                     lambda b: w2_r[:, b, hc, :], hc == 0 and j % 2 == 0, hc == FC - 1, skip_group_check=True)
                last.then_inc(s["ys_psum"], 1)

            def slot_step(sl, par):
                layer1(sl)
                if within(sl + 1, NS):
                    slot_transposes(sl + 1, 1 - par)
                layer2(sl)

            pe.wait_ge(s["o_done"], NT)
            slot_transposes(0, 0)
            run_steps(pe, 0, NS, 2, NS - 1, slot_step)

        @block.vector
        def _(dve):
            nc.vector.memset(eps_col[:], EPS).then_inc(s["tri_done"], 1)
            nc.vector.memset(ident_bf[:, 0], 1.0).then_inc(s["tri_done"], 1)
            nc.vector.memset(state_f, 0.0).then_inc(s["st_zero"], 1)
            dve.wait_ge(s["consts_in"], 16)
            nc.vector.tensor_tensor(ident_bf[:, 1], C["causal"], ident, ALU.subtract).then_inc(s["tri_done"], 1)
            dve.wait_ge(s["small_in"], 80)

            def ln_stats(g, par):
                dve.wait_ge(s[f"x_in{par}"], (g - par) * 8 + 16)
                for t in range(GRP):
                    nc.vector.bn_stats(stats[:, par, t], x_raw[:, par, t]).then_inc(s["ln_stats"], 1)
                dve.wait_ge(s["ln_stats"], GRP * (g + 1))
                nc.vector.tensor_copy(fence_d[:, 0:1], eps_col[:])
                for t in range(GRP):
                    last = nc.vector.bn_aggr(mean_var[:, par, t], stats[:, par, t])
                last.then_inc(s["ln_var"], 1)

            def ln_norm(g, par):
                dve.wait_ge(s["ln_std"], g + 1)
                nc.vector.reciprocal(rstd[:, par], std[:, par]).then_inc(s["ln_rstd"], 1)
                dve.wait_ge(s["ln_rstd"], g + 1)
                wait(dve, s["ln_t_psum"], KC * (g - 1))
                wait(dve, s["ln_xn"], g - 1)
                for t in range(GRP):
                    last = nc.vector.tensor_scalar(x_grp[:, par, t], x_raw[:, par, t], mean_var[:, par, t, 0:1], rstd[:, par, t:t + 1],
                                                   ALU.subtract, ALU.mult)
                last.then_inc(s["ln_xg"], 1)

            def ln_logit(g, par):
                dve.wait_ge(s["ln_logit_psum"], g + 1)
                nc.vector.tensor_tensor(logits[:, bass.ds(g * GRP, GRP), :], ps[:, 4 + par, 0:GRP * E].rearrange("p (t e) -> p t e", t=GRP),
                                        gate_bias[:].unsqueeze(1).to_broadcast([P, GRP, E]), ALU.add).then_inc(s["ln_logit"], 1)

            def ln_step(g, par):
                if within(g + 1, NG):
                    ln_stats(g + 1, 1 - par)
                if within(g, NG):
                    ln_norm(g, par)
                if within(g - 1, NG):
                    ln_logit(g - 1, 1 - par)

            run_steps(dve, -1, NG + 1, 2, NG - 2, ln_step)

            count = [0]

            def chained(ins, n=1):
                count[0] += 1
                ins.then_inc(s["dve_route"], 1)
                dve.wait_ge(s["dve_route"], count[0])

            def over_e(a):
                return a.unsqueeze(2).to_broadcast([P, NT, E])

            def over_t(a):
                return a.unsqueeze(1).to_broadcast([P, NT, E])

            V = nc.vector
            rest, shifted, probs, first, second, tmp = rt
            peak, total, one, gate_sum = rs[:, 0], rs[:, 1], rs[:, 2], rs[:, 3]
            dve.wait_ge(s["ln_logit"], NG)
            chained(V.tensor_reduce(peak, logits[:], AX, ALU.max))
            V.tensor_tensor(shifted, logits[:], over_e(peak), ALU.subtract).then_inc(s["route"], 1)

            def first_of_max(onehot, scores_, peak_):
                chained(V.tensor_tensor(tmp, scores_, over_e(peak_), ALU.is_equal))
                chained(V.tensor_tensor(tmp, tmp, over_t(C["rank_low"]), ALU.mult))
                chained(V.tensor_reduce(one, tmp, AX, ALU.max))
                chained(V.tensor_tensor(onehot, tmp, over_e(one), ALU.is_equal))

            first_of_max(first, logits[:], peak)
            chained(V.scalar_tensor_tensor(rest, first, -BIG, logits[:], ALU.mult, ALU.add))
            chained(V.tensor_reduce(peak, rest, AX, ALU.max))
            first_of_max(second, rest, peak)
            chained(V.tensor_tensor(tmp, first, second, ALU.add))
            V.tensor_copy(mask_bf[:], tmp.rearrange("p t e -> p (t e)")).then_inc(s["route_mask"], 1)
            dve.wait_ge(s["route_exp"], 1)
            chained(V.tensor_reduce(total, probs, AX, ALU.add))
            chained(V.reciprocal(total, total))
            chained(V.tensor_tensor(probs, probs, over_e(total), ALU.mult))
            chained(V.tensor_tensor(gates[:], probs, tmp, ALU.mult))
            for k, onehot in enumerate((first, second)):
                chained(V.tensor_tensor(tmp, probs, onehot, ALU.mult))
                chained(V.tensor_reduce(gate2[:, :, k], tmp, AX, ALU.add))
            dve.wait_ge(s["route_psum"], 1)
            by_expert = rest.rearrange("p t e -> p (t e)").rearrange("p (e t) -> p e t", e=E)
            upto = shifted.rearrange("p t e -> p (t e)").rearrange("p (e t) -> p e t", e=E)
            chained(V.tensor_copy(by_expert, ps[:, 6, 0:NT * E].rearrange("p (t e) -> p e t", t=NT)))
            chained(V.memset(tmp, 1.0))
            chained(V.tensor_tensor_scan(upto.rearrange("p e t -> p (e t)"), tmp.rearrange("p t e -> p (t e)"),
                                         by_expert.rearrange("p e t -> p (e t)"), 0.0, ALU.mult, ALU.add))
            tokens, slots, slot_end, base, ones_e, before = (re[:, i] for i in range(6))
            last_t = upto[:, :, NT - 1]
            chained(V.memset(before[:, 0:1], 0.0))
            chained(V.tensor_copy(before[:, 1:E], last_t[:, 0:E - 1]))
            chained(V.tensor_tensor(tokens, last_t, before, ALU.subtract))
            chained(V.tensor_tensor(rk[:], tokens.unsqueeze(2).to_broadcast([P, E, NK]),
                                    C["slot_rows"].unsqueeze(1).to_broadcast([P, E, NK]), ALU.is_gt))
            chained(V.tensor_reduce(slots, rk[:], AX, ALU.add))
            chained(V.memset(ones_e, 1.0))
            chained(V.tensor_tensor_scan(slot_end, ones_e, slots, 0.0, ALU.mult, ALU.add))
            chained(V.tensor_tensor(base, slot_end, slots, ALU.subtract))
            chained(V.scalar_tensor_tensor(base, base, float(SLOT), before, ALU.mult, ALU.subtract))
            chained(V.tensor_tensor(upto, upto, by_expert, ALU.subtract))
            chained(V.tensor_tensor(upto, upto, base.unsqueeze(2).to_broadcast([P, E, NT]), ALU.add))
            chained(V.tensor_tensor(rest, ps[:, 7, 0:NT * E].rearrange("p (t e) -> p t e", t=NT),
                                    upto.rearrange("p e t -> p t e"), ALU.add))
            for k, onehot in enumerate((first, second)):
                chained(V.tensor_tensor(tmp, rest, onehot, ALU.mult))
                chained(V.tensor_reduce(rs[:, 4 + k], tmp, AX, ALU.add))
                chained(V.tensor_copy(rows2[:, :, k], rs[:, 4 + k]))
            chained(V.tensor_tensor(rse, C["slot_no"].unsqueeze(2).to_broadcast([P, NS, E]),
                                    slot_end.unsqueeze(1).to_broadcast([P, NS, E]), ALU.is_ge))
            chained(V.tensor_reduce(rs[:, 6, 0:NS], rse, AX, ALU.add))
            chained(V.tensor_scalar(rs[:, 6, 0:NS], rs[:, 6, 0:NS], float(E - 1), None, ALU.min))
            V.tensor_copy(expert_of[:], rs[:, 6, 0:NS]).then_inc(s["route_done"], 1)
            chained(V.tensor_tensor(rse, C["expert_no"].unsqueeze(1).to_broadcast([P, NS, E]),
                                    rs[:, 6, 0:NS].unsqueeze(2).to_broadcast([P, NS, E]), ALU.is_equal))
            chained(V.tensor_tensor(rsl, b1_sb[:].unsqueeze(1).to_broadcast([P, NS, FC, E]),
                                    rse.unsqueeze(2).to_broadcast([P, NS, FC, E]), ALU.mult))
            V.tensor_reduce(b1_slot[:], rsl, AX, ALU.add).then_inc(s["b1_done"], 1)
            dve.wait_ge(s["b1_done"], 1)
            dve.wait_ge(s["route_done"], 1)

            def chunk(i, par):
                if within(i, NT):
                    for g in range(RG):
                        m = RG * i + g
                        dve.wait_ge(s["s_psum"], RG * i + 2 * (g // 2) + 2)
                        wait(dve, s["s_h"], m - 1)
                        wait(dve, s["s_l"], m - 1)
                        V.tensor_tensor(s_f[:, g % 2].rearrange("p (h i) -> p h i", h=4),
                                        ps[:, g, :].rearrange("p (h i) -> p h i", h=4),
                                        C["causal"].unsqueeze(1).to_broadcast([P, 4, P]), ALU.mult).then_inc(s["s_f"], 1)
                n, np_ = i + 1, 1 - par
                if within(n, NT):
                    dve.wait_ge(s["kv_psum"], n + 1)
                    wait(dve, s["k_l"], n - 1)
                    wait(dve, s["k_h"], n - 1)
                    wait(dve, s["kt_psum"], n - 1)
                    V.tensor_tensor(k_f[:, np_], ps[:, 4, 0:D], C["tab_k"], ALU.mult).then_inc(s["k_f"], 1)
                    dve.wait_ge(s["q_psum"], n + 1)
                    wait(dve, s["q_l"], n - 1)
                    wait(dve, s["q_h"], n - 1)
                    V.tensor_tensor(q_f[:, np_], ps[:, 5, 0:256].rearrange("p (c i) -> p c i", c=KC), tab_q, ALU.mult).then_inc(s["q_f"], 1)
                    dve.wait_ge(s["v_h"], n + 1)
                    wait(dve, s["y_psum"], n - 1)
                    V.tensor_tensor(v_r[:, np_, 1], ps[:, 4, D:2 * D], v_r[:, np_, 0].bitcast(F32), ALU.subtract).then_inc(s["v_l"], 1)
                if within(i - 1, NT):
                    m = i - 1
                    dve.wait_ge(s["u_psum"], m + 1)
                    wait(dve, s["st_f"], m)
                    V.tensor_tensor(state_t, ps[:, 6, 256:512].rearrange("p (c i) -> p c i", c=KC), state_f, ALU.add).then_inc(s["st_t"], 1)
                    dve.wait_ge(s["st_t"], m + 1)
                    wait(dve, s["st_h"], m)
                    wait(dve, s["st_l"], m)
                    V.scalar_tensor_tensor(state_f, state_t, C["keep"][:, bass.ds(m + 1, 1)], decay, ALU.mult, ALU.mult).then_inc(s["st_f"], 1)
                if within(n, NT):
                    dve.wait_ge(s["kt_psum"], n + 1)
                    wait(dve, s["s_psum"], RG * (n - 1))
                    dve.wait_ge(s["keo_h"], 2 * n + 2)
                    for odd in range(2):
                        V.scalar_tensor_tensor(keo[:, np_, 2 + odd], ps[:, 5, 0:256], C["parity"][:, odd:odd + 1],
                                               keo[:, np_, odd].bitcast(F32), ALU.mult, ALU.subtract).then_inc(s["keo_l"], 1)
                if within(i + 2, NT):
                    m = i + 2
                    dve.wait_ge(s["xt_h"], m + 1)
                    wait(dve, s["q_psum"], m - 1)
                    V.tensor_tensor(xt[:, par, 1], ps[:, 4, 0:256], xt[:, par, 0].bitcast(F32), ALU.subtract).then_inc(s["xt_l"], 1)

            run_steps(dve, -2, NT + 1, 4, 28, chunk)
            dve.wait_ge(s["y_t"], NT)

            def norm_batch(b):
                def gn(ins, k):
                    ins.then_inc(s["gn_chain"], 1)
                    dve.wait_ge(s["gn_chain"], b * 7 + k)

                for c in range(KC):
                    for half in range(2):
                        last = V.bn_stats(bstat[:, c, half], y_t[:, c, bass.ds(b * T + half * 512, 512)])
                gn(last, 1)
                nc.vector.tensor_copy(fence_d[:, 0:1], eps_col[:])
                for c in range(KC):
                    last = V.bn_aggr(bmv[:, c], bstat[:, c].rearrange("p a b -> p (a b)"))
                gn(last, 2)
                V.tensor_tensor(bsm[:, 4], bmv[:, :, 0], bmv[:, :, 0], ALU.mult).then_inc(s["gn_chain"], 1)
                dve.wait_ge(s["gn_chain"], b * 7 + 3)
                V.tensor_copy(bsm[:, 0], bmv[:, :, 0]).then_inc(s["gn_chain"], 1)
                V.tensor_tensor(bsm[:, 1], bsm[:, 4], bmv[:, :, 1], ALU.add).then_inc(s["gn_chain"], 1)
                dve.wait_ge(s["gn_avg_psum"], b + 1)
                V.tensor_copy(bsm[:, 0:2].rearrange("p a c -> p (a c)"), ps[:, 5, 0:2 * KC]).then_inc(s["gn_chain"], 1)
                dve.wait_ge(s["gn_chain"], b * 7 + 6)
                V.tensor_tensor(bsm[:, 4], bsm[:, 0], bsm[:, 0], ALU.mult).then_inc(s["gn_chain"], 1)
                dve.wait_ge(s["gn_chain"], b * 7 + 7)
                V.tensor_tensor(bsm[:, 2], bsm[:, 1], bsm[:, 4], ALU.subtract).then_inc(s["gn_mv"], 1)
                dve.wait_ge(s["gn_std"], b + 1)
                V.reciprocal(bsm[:, 3], bsm[:, 3]).then_inc(s["f_x"], 1)
                dve.wait_ge(s["f_x"], b * 3 + 1)
                V.tensor_tensor(bsm[:, 5], bsm[:, 3], gn_sb[:, 0], ALU.mult).then_inc(s["f_x"], 1)
                dve.wait_ge(s["f_x"], b * 3 + 2)
                V.tensor_tensor(bsm[:, 7], bsm[:, 0], bsm[:, 5], ALU.mult).then_inc(s["f_x"], 1)
                dve.wait_ge(s["f_x"], b * 3 + 3)
                V.tensor_tensor(bsm[:, 6], gn_sb[:, 1], bsm[:, 7], ALU.subtract).then_inc(s["gn_ab"], 1)
                for half in range(2):
                    hb = b * 2 + half
                    wait(dve, s["g4_psum"], hb)
                    V.tensor_copy(gate_b4[:], gates[:, bass.ds(hb * 4, 4), :]).then_inc(s["g4"], 1)
                    dve.wait_ge(s["yn_h"], hb + 1)
                    V.tensor_tensor(yn_r[:, 1], yn_f, yn_r[:, 0].bitcast(F32), ALU.subtract).then_inc(s["yn_l"], 1)
                    dve.wait_ge(s["x_res_in"], hb * 16 + 16)
                    for t in range(4):
                        dve.wait_ge(s["o_psum"], hb * 4 + t + 1)
                        V.tensor_tensor(part_out[:, bass.ds(hb * 4 + t, 1), :].rearrange("p a d -> p (a d)"), ps[:, t, 0:D],
                                        x_res[:, t], ALU.add).then_inc(s["o_done"], 1)

            run_batches(dve, B, norm_batch)

            def xs_low(sl):
                dve.wait_ge(s["xst_h"], sl + 1)
                V.tensor_tensor(xs_r[:, 1].rearrange("p (k n) -> p k n", k=KC), ps[:, 0:2, :],
                                xs_r[:, 0].rearrange("p (k n) -> p k n", k=KC).bitcast(F32), ALU.subtract).then_inc(s["xst_l"], 1)

            def ys_copy(sl):
                dve.wait_ge(s["ys_psum"], sl + 1)
                wait(dve, s["ys_out"], 16 * sl)
                V.tensor_copy(ys, ps[:, 6:8, :].rearrange("p a b -> p (a b)")).then_inc(s["ys_sb"], 1)

            def slot_step(sl, par):
                for hc in range(FC):
                    m = sl * FC + hc
                    dve.wait_ge(s["h_f"], m + 1)
                    wait(dve, s["ys_psum"], sl)
                    V.tensor_copy(h_r[:, 0, hc], h_f[:, hc % 2]).then_inc(s["h_h"], 1)
                    if hc == 0 and within(sl - 1, NS):
                        ys_copy(sl - 1)
                    dve.wait_ge(s["h_h"], m + 1)
                    V.tensor_tensor(h_r[:, 1, hc], h_f[:, hc % 2], h_r[:, 0, hc].bitcast(F32), ALU.subtract).then_inc(s["h_l"], 1)
                if within(sl + 1, NS):
                    xs_low(sl + 1)

            xs_low(0)
            run_steps(dve, 0, NS, 2, NS - 1, slot_step)
            ys_copy(NS - 1)

            def token_tile(t, b4, rounds, store):
                dve.wait_ge(s[f"pair{b4}"], rounds)
                wait(dve, s["out_done"], store)
                V.scalar_tensor_tensor(out_sb[:, b4], y_pair[b4][:, 0], gate2[:, bass.ds(t, 1), 0], part_out[:, bass.ds(t, 1), :].rearrange("p a d -> p (a d)"),
                                       ALU.mult, ALU.add).then_inc(s["f_a"], 1)
                dve.wait_ge(s["f_a"], t + 1)
                V.scalar_tensor_tensor(out_sb[:, b4], y_pair[b4][:, 1], gate2[:, bass.ds(t, 1), 1], out_sb[:, b4],
                                       ALU.mult, ALU.add).then_inc(s["f_b"], 1)

            def four_tiles(t4):
                for b4 in range(4):
                    token_tile(t4 * 4 + b4, b4, t4 * 32 + 32, t4 * 16)

            run_batches(dve, NT // 4, four_tiles)


def kernel(L0_attn_x, L0_attn_W_q, L0_attn_W_k, L0_attn_W_v, L0_attn_W_o, L0_attn_gn_weight, L0_attn_gn_bias,
           L0_ffn_gate_w, L0_ffn_gate_b, L0_ffn_w1, L0_ffn_b1, L0_ffn_w2, L0_ffn_b2):
    import concourse.bacc as bacc
    from concourse.bass_utils import run_bass_kernel_spmd

    const, where = constants()
    a = np.asarray
    gn = np.stack([a(L0_attn_gn_weight).reshape(KC, P), a(L0_attn_gn_bias).reshape(KC, P)]).transpose(2, 0, 1)
    arrays = {
        "x": a(L0_attn_x),
        "wq_t": a(L0_attn_W_q).T,
        "wkv_t": np.concatenate([a(L0_attn_W_k).T, a(L0_attn_W_v).T], 1),
        "wo_t": a(L0_attn_W_o).T,
        "gn": gn,
        "gate_t": a(L0_ffn_gate_w).T,
        "gate_b": a(L0_ffn_gate_b),
        "w1": a(L0_ffn_w1).reshape(E, KC, P, F).transpose(0, 2, 1, 3).reshape(E, P, KC * F),
        "w2": a(L0_ffn_w2).reshape(E, FC, P, D).transpose(0, 2, 1, 3).reshape(E, P, FC * D),
        "b1_t": a(L0_ffn_b1).reshape(E, FC, P).transpose(2, 1, 0),
        "b2": a(L0_ffn_b2),
        "const": const,
    }
    arrays = {k: np.ascontiguousarray(v) for k, v in arrays.items()}
    nc = bacc.Bacc("TRN2", target_bir_lowering=False, num_devices=1)
    args = {k: nc.dram_tensor(k, v.shape, mybir.dt.from_np(v.dtype), kind="ExternalInput").ap() for k, v in arrays.items()}
    out = nc.dram_tensor("out", (B, T, D), F32, kind="ExternalOutput").ap()
    build(nc, where, out=out, **args)
    r = run_bass_kernel_spmd(nc, [arrays], core_ids=[0])
    return r.results[0]["out"]
```

```python
from contextlib import ExitStack

import numpy as np

import concourse.bass as bass
from concourse import mybir

F32 = mybir.dt.float32
FR = mybir.dt.float32r
BF16 = mybir.dt.bfloat16
I32 = mybir.dt.int32
ALU = mybir.AluOpType
ACT = mybir.ActivationFunctionType
AX = mybir.AxisListType.X

P = 128
B, T, D = 4, 1024, 256
KC = D // P
NT = B * T // P
CB = T // P
H, DH = 16, 16
HP = P // DH
HB = 4
NB = H // HB
E, F = 8, 1024
FC = F // P
SLOT = 256
SJ = SLOT // P
NS = (2 * NT * P - E) // SLOT + E
NK = NT * P // SLOT
EPS = 1e-5
GRP = 4
NG = NT // GRP
BIG = 1e30
W2_POOL = 1536
W = D + 2

PASSES = ((0, 0), (0, 1), (1, 0))


def constants():
    i = np.arange(P)
    gam = 1.0 - 2.0 ** (-5.0 - np.arange(H, dtype=np.float64))
    head = (np.arange(D) // DH)
    local = (i % P) // DH
    tab_q = gam[head][None, :] ** (i[:, None] - 64.0) / np.sqrt(DH)
    same = local[:, None] == local[None, :]
    decay = np.stack([same * (gam[c * HP + local] ** P)[:, None] for c in range(KC)], 1)
    keep = np.ones((P, NT + 1))
    keep[:, ::CB] = 0.0
    cols = {
        "ident": np.eye(P),
        "causal": (i[None, :] >= i[:, None]) * 1.0,
        "tab_q": tab_q,
        "tab_k": gam[head][None, :] ** (64.0 - i[:, None]),
        "decay": decay.reshape(P, -1),
        "group_mean": same / DH,
        "keep": keep,
        "slot_rows": np.tile(np.arange(NK) * float(SLOT), (P, 1)),
        "slot_no": np.tile(np.arange(NS) * 1.0, (P, 1)),
        "pair_no": (np.arange(NT)[None, :, None] * P + i[:, None, None]).repeat(2, 2).reshape(P, -1) * 2.0
        + np.tile([0.0, 1.0], NT),
        "spare_no": 2.0 * NT * P + i[:, None] * SJ + np.arange(SJ)[None, :],
        "rank_low": np.tile(E - np.arange(E) * 1.0, (P, 1)),
    }
    at, where = 0, {}
    for name, a in cols.items():
        where[name] = (at, at + a.shape[1])
        at += a.shape[1]
    return np.concatenate(list(cols.values()), 1).astype(np.float32), where


def run_steps(eng, first, last, lo, hi, step):
    for i in range(first, lo):
        step(i, i % 2)
    assert lo % 2 == 0 and hi % 2 == 0
    with eng.Fori(lo // 2, hi // 2) as pair:
        step(pair * 2, 0)
        step(pair * 2 + 1, 1)
    for i in range(hi, last):
        step(i, i % 2)


def run_batches(eng, count, batch):
    batch(0)
    with eng.Fori(1, count) as b:
        batch(b)


def within(n, count):
    return not isinstance(n, int) or 0 <= n < count


def wait(eng, sem, value):
    if isinstance(value, int) and value <= 0:
        return
    eng.wait_ge(sem, value)


def build(nc, where, x, wq_t, wkv_t, wo_t, gn, gate_t, gate_b, w1, w2, b1, b2, const, out):
    xs_rows = nc.dram_tensor("xs_rows", [NS * SLOT, W], F32).ap()
    pair_rows = nc.dram_tensor("pair_rows", [2 * NT * P + SLOT, D], F32).ap()
    pair_tiles = pair_rows[0:2 * NT * P].rearrange("(t p k) d -> p t (k d)", p=P, k=2)
    x_tiles = x.rearrange("b (c p) d -> p (b c) d", p=P)
    out_tiles = out.rearrange("b (c p) d -> p (b c) d", p=P)
    xs_slots = xs_rows.rearrange("(s p j) d -> s p j d", p=P, j=SJ)

    with ExitStack() as ctx:
        def sb(name, shape, dt=F32):
            return ctx.enter_context(nc.sbuf_tensor(name, shape, dt))

        def sem(name):
            return ctx.enter_context(nc.semaphore(name))

        class Arena:

            def __init__(self, name, words, dt):
                self.t, self.words, self.at = sb(name, [P, words], dt), words, 0

            def __call__(self, *dims):
                n = int(np.prod(dims))
                a = self.t[:, self.at:self.at + n]
                self.at += n
                assert self.at <= self.words, (self.at, self.words)
                names = "abcd"[:len(dims)]
                if len(dims) > 1:
                    a = a.rearrange(f"p ({' '.join(names)}) -> p {' '.join(names)}",
                                    **{k: v for k, v in zip(names, dims)})
                return a

        cst = sb("cst", [P, const.shape[1]])
        C = {k: cst[:, a:b] for k, (a, b) in where.items()}
        ident = C["ident"]
        decay = C["decay"].rearrange("p (c i) -> p c i", c=KC)
        xn = sb("xn", [P, NT, D])
        y_t = xn[:].rearrange("p t (c i) -> p t c i", c=KC)
        wq = sb("wq", [P, 2, KC, D], FR)
        wkv = sb("wkv", [P, 2, KC, 2 * D], FR)
        wo = sb("wo", [P, 2, KC, D], FR)
        gn_sb = sb("gn_sb", [P, 2, KC])
        gate_w = sb("gate_w", [P, KC, E])
        gate_bias = sb("gate_bias", [P, E])
        pair_info = sb("pair_info", [P, NT, 2, 2])
        rows2 = sb("rows2", [P, NT, 2], I32)
        expert_of = sb("expert_of", [P, NS], I32)
        logits = sb("logits", [P, NT, E])
        ident_bf = sb("ident_bf", [P, 2, P], BF16)
        mask_bf = sb("mask_bf", [P, NT * E], BF16)
        eps_col = sb("eps_col", [P, 1])
        fence_d = sb("fence_d", [P, 1])
        fence_p = sb("fence_p", [P, 1])
        spare_rows = sb("spare_rows", [P, SJ, W])

        fr = Arena("arena_r", 22016, FR)
        ff = Arena("arena_f", 12288, F32)

        w_raw = [ff(KC * cols) for cols in (D, 2 * D, D)]
        x_grp = ff(2, GRP, D)
        x_grp_t = ff(2, KC, GRP * P)
        stats = sb("stats", [P, 2, GRP, 6])
        mean_var = sb("mean_var", [P, 2, GRP, 2])
        std = sb("std", [P, 2, GRP])
        rstd = sb("rstd", [P, 2, GRP])
        rt = [ff(NT, E) for _ in range(6)]
        rs = sb("rs", [P, 6, NT])
        slot_expert = sb("slot_expert", [P, NS])
        re = sb("re", [P, 6, E])
        rk = sb("rk", [P, E, NK])
        rse = ff(NS, E)
        ff.at = 0
        x_chunk = [sb(f"x_chunk{i}", [P, D]) for i in range(2)]
        pair_chunk = [sb(f"pair_chunk{i}", [P, 2, W]) for i in range(2)]
        row_chunk = [sb(f"row_chunk{i}", [P, 2], I32) for i in range(2)]
        kq_f = ff(2, 2 * D)
        v_f = ff(2, D)
        s_f = ff(NB, HB * P)
        y_f = ff(2, D)
        state_f = ff(KC, P)
        state_t = ff(KC, P)
        xt = fr(2, 2, KC * P)
        k_r = fr(2, 2, D)
        v_r = fr(2, H, 2, DH)
        kq_t = fr(2, 2, 2, KC * P)
        q_diag = fr(2, 2, KC, HP * P)
        s_r = fr(2, 2, NB, HB * P)
        state_r = fr(2, KC * P)
        y_stats = sb("y_stats", [P, KC, NT, 6])
        ff.at = fr.at = 0
        w1_raw = ff(2, KC * F)
        w2_raw = ff(2, FC * D)
        xs = ff(2, SJ, D)
        h_f = ff(2, 2 * SLOT)
        ys = ff(SJ * D)
        b1_slot = ff(2, FC)
        b2_slot = ff(2, D)
        pair_slot = ff(2, SJ, 2)
        w1_r = fr(2, 2, KC * F)
        w2_r = fr(2, 2, FC * D)
        h_r = fr(2, FC * SLOT)
        xs_r = fr(2, KC * SLOT)
        ff.at = fr.at = 0
        y_pair = ff(2, 4, 2, D)
        yn_f = ff(2, KC, 4 * P)
        x_res = ff(2, 4, D)
        out_sb = ff(2, 4, D)
        yn_r = fr(2, 2, KC, 4 * P)
        y_sum = ff(2, 4, D)
        y_mv = sb("y_mv", [P, B, KC, 2])
        gn_t = sb("gn_t", [P, 8, B, KC])
        gn_ab = sb("gn_ab", [P, 2, B, 2, KC])

        ps = ctx.enter_context(nc.psum_tensor("ps", [P, 8, 512], F32))

        s = {}
        for name in (
            "consts_in wq_in wkv_in wo_in small_in w_split_h w_split_l zeroed rows_zero "
            "x_in0 x_in1 x_in2 x_in3 x_in4 x_in5 x_in6 x_in7 ln_stats ln_var ln_std ln_rstd ln_xg ln_t_psum ln_t_sb ln_logit_psum ln_logit ln_xn "
            "route dve_route route_exp route_mask route_psum rows_done route_done tri_done "
            "xc0 xc1 rc0 rc1 xt_psum xt_h xt_l kv_psum q_psum k_f k_h k_l v_f v_h v_l q_f kqt_psum kqt_h kqt_l q_diag0 q_diag1 "
            "s_psum s_f s_h s_l_pool s_l_dve y_psum across_done u_psum st_t st_f st_h st_l y_f yt_psum y_t y_stats "
            "fence scat0 scat1 r_zero "
            "gn_chain gn_avg_psum gn_var gn_std gn_ab yn_f yn_h yn_l o_psum x_res_in0 x_res_in1 "
            "xs_in0 xs_in1 bias_in0 bias_in1 w1_in0 w1_in1 w2_in0 w2_in1 w1_h w1_l w2_h w2_l xst_psum xst_h xst_l "
            "h_psum h_f h_h h_l ys_psum ys_sum ys_sb pair_slot0 pair_slot1 w2_l_dve pairs_out spare y_sum y_res out_sb out_done0 out_done1 "
            "pair_in0 pair_in1"
        ).split():
            s[name] = sem(name)

        block = ctx.enter_context(nc.Block())

        @block.sync
        def _(sp):
            def ln_load(g):
                tiles = slice(g * GRP, (g + 1) * GRP)
                sp.dma_start(xn[:, tiles, :], x_tiles[:, tiles, :]).then_inc(s[f"x_in{g}"], 16)

            ln_load(0)
            sp.dma_start(cst[:], const).then_inc(s["consts_in"], 16)
            sp.dma_start(gate_w[:], gate_t.rearrange("(k p) e -> p k e", p=P)).then_inc(s["small_in"], 16)
            sp.dma_start(gate_bias[:], gate_b.rearrange("(a e) -> a e", a=1).to_broadcast([P, E])).then_inc(s["small_in"], 16)
            sp.dma_start(gn_sb[:], gn).then_inc(s["small_in"], 16)
            for g in range(1, NG):
                ln_load(g)
            for k, (src, name) in enumerate(((wq_t, "wq_in"), (wkv_t, "wkv_in"), (wo_t, "wo_in"))):
                sp.dma_start(w_raw[k].rearrange("p (k n) -> p k n", k=KC),
                             src.rearrange("(k p) n -> p k n", p=P)).then_inc(s[name], 16)
            sp.wait_ge(s["spare"], 1)
            with sp.Fori(0, NS) as sl:
                sp.dma_start(xs_slots[bass.ds(sl, 1)].rearrange("a p j d -> (a p) (j d)"),
                             spare_rows[:].rearrange("p j d -> p (j d)")).then_inc(s["rows_zero"], 16)

            def tokens_stage(n, par):
                sp.dma_start(x_chunk[par][:], xn[:, bass.ds(n, 1), :].rearrange("p a d -> p (a d)")).then_inc(s[f"xc{par}"], 16)

            def pairs_stage(n, par):
                sp.dma_start(pair_chunk[par][:, :, 0:D], xn[:, bass.ds(n, 1), :].to_broadcast([P, 2, D])).then_inc(s[f"rc{par}"], 16)
                sp.dma_start(pair_chunk[par][:, :, D:W], pair_info[:, bass.ds(n, 1)].rearrange("p a k w -> p (a k) w")).then_inc(s[f"rc{par}"], 16)
                sp.dma_start(row_chunk[par][:], rows2[:, bass.ds(n, 1), :].rearrange("p a d -> p (a d)")).then_inc(s[f"rc{par}"], 16)

            def queries_to_diagonal(n, par):
                wait(sp, s["s_psum"], NB * (n - 1))
                sp.wait_ge(s["kqt_h"], n + 1)
                sp.wait_ge(s["kqt_l"], n + 1)
                for h in range(HP):
                    r = slice(h * DH, (h + 1) * DH)
                    sp.dma_start(q_diag[r, par, :, :, h * P:(h + 1) * P].bitcast(F32).rearrange("p s c i -> p (s c) i"),
                                 kq_t[r, par, 1].bitcast(F32).rearrange("p s (c i) -> p (s c) i", c=KC)).then_inc(s[f"q_diag{par}"], 16)

            sp.wait_ge(s["ln_xn"], 1)
            tokens_stage(0, 0)
            tokens_stage(1, 1)
            sp.wait_ge(s["r_zero"], 3)
            queries_to_diagonal(0, 0)
            sp.wait_ge(s["rows_done"], 2)
            pairs_stage(0, 0)
            pairs_stage(1, 1)
            sp.wait_ge(s["ln_xn"], NG)
            sp.wait_ge(s["xt_psum"], 1)
            tokens_stage(2, 0)

            def chunk_step(i, par):
                if within(i + 3, NT):
                    wait(sp, s["xt_psum"], i + 2)
                    tokens_stage(i + 3, 1 - par)
                if within(i + 1, NT):
                    queries_to_diagonal(i + 1, 1 - par)
                if within(i + 2, NT):
                    wait(sp, s[f"scat{par}"], (i - par) * 16 + 32)
                    pairs_stage(i + 2, par)

            run_steps(sp, 0, NT, 4, 28, chunk_step)

            sp.wait_ge(s["route_done"], 1)
            for par in range(2):
                sp.wait_ge(s[f"scat{par}"], 16 * NT)
            sp.wait_ge(s["y_t"], NT)
            sp.wait_ge(s["st_l"], NT)

            def expert(sl):
                return bass.ds(sp.value_load(expert_of[0:1, bass.ds(sl, 1)], min_val=0, max_val=E - 1), 1)

            def slot_load(sl, par):
                e = expert(sl)
                wait(sp, s["w1_h"], sl - 1)
                wait(sp, s["w1_l"], sl - 1)
                sp.dma_start(w1_raw[:, par], w1[e].rearrange("a p n -> (a p) n")).then_inc(s[f"w1_in{par}"], 16)
                wait(sp, s["xst_psum"], sl - 1)
                sp.dma_start(xs[:, par], xs_slots[bass.ds(sl, 1), :, :, 0:D].rearrange("a p j d -> (a p) j d")).then_inc(s[f"xs_in{par}"], 16)
                wait(sp, s["w2_h"], sl - 1)
                wait(sp, s["w2_l"], sl - 1)
                wait(sp, s["w2_l_dve"], sl - 1)
                sp.dma_start(w2_raw[:, par], w2[e].rearrange("a p n -> (a p) n")).then_inc(s[f"w2_in{par}"], 16)

            def bias_load(sl, par):
                e = expert(sl)
                wait(sp, s["ys_sb"], sl - 1)
                sp.dma_start(b1_slot[:, par], b1[e].rearrange("a p n -> (a p) n")).then_inc(s[f"bias_in{par}"], 16)
                sp.dma_start(b2_slot[:, par], b2[e].to_broadcast([P, D])).then_inc(s[f"bias_in{par}"], 16)

            def pair_load(sl, par):
                wait(sp, s["pairs_out"], 32 * (sl - 1))
                sp.dma_start(pair_slot[:, par], xs_slots[bass.ds(sl, 1), :, :, D:W].rearrange("a p j d -> (a p) j d")).then_inc(s[f"pair_slot{par}"], 16)

            slot_load(0, 0)
            bias_load(0, 0)
            pair_load(0, 0)
            slot_load(1, 1)

            def slot_step(sl, par):
                if within(sl + 2, NS):
                    slot_load(sl + 2, par)
                if within(sl + 1, NS):
                    bias_load(sl + 1, 1 - par)
                    pair_load(sl + 1, 1 - par)

            run_steps(sp, 0, NS - 1, 2, NS - 3, slot_step)

            sp.wait_ge(s["pairs_out"], 32 * NS)

            def residual_load(hb, par):
                wait(sp, s["y_res"], hb - 1)
                sp.dma_start(y_pair[:, par].rearrange("p t k d -> p t (k d)"), pair_tiles[:, bass.ds(hb * 4, 4), :]).then_inc(s[f"pair_in{par}"], 16)
                sp.dma_start(x_res[:, par], x_tiles[:, bass.ds(hb * 4, 4), :]).then_inc(s[f"x_res_in{par}"], 16)

            residual_load(0, 0)
            residual_load(1, 1)

            def out_store(hb, par):
                if within(hb + 2, 2 * B):
                    residual_load(hb + 2, par)
                sp.wait_ge(s["out_sb"], hb + 1)
                sp.dma_start(out_tiles[:, bass.ds(hb * 4, 4), :], out_sb[:, par]).then_inc(s[f"out_done{par}"], 16)

            run_steps(sp, 0, 2 * B, 0, 2 * B - 2, out_store)
            for par in range(2):
                sp.wait_ge(s[f"out_done{par}"], 16 * B)
            sp.wait_ge(s["rows_zero"], 16 * NS)

        @block.gpsimd
        def _(pool):
            nc.gpsimd.memset(spare_rows[:], 0.0).then_inc(s["zeroed"], 1)
            nc.gpsimd.memset(state_r.bitcast(F32), 0.0).then_inc(s["r_zero"], 1)
            for par in range(2):
                nc.gpsimd.memset(q_diag[:, par].bitcast(F32), 0.0).then_inc(s["r_zero"], 1)
            pool.wait_ge(s["consts_in"], 16)
            pool.wait_ge(s["zeroed"], 1)
            nc.gpsimd.tensor_copy(spare_rows[:, :, D:D + 1].bitcast(I32), C["spare_no"].unsqueeze(2)).then_inc(s["spare"], 1)
            for n, dst in enumerate((wq, wkv, wo)):
                pool.wait_ge(s["w_split_h"], n + 1)
                flat = dst[:].rearrange("p s k n -> p s (k n)")
                nc.gpsimd.tensor_tensor(flat[:, 1], w_raw[n], flat[:, 0].bitcast(F32), ALU.subtract).then_inc(s["w_split_l"], 1)
            pool.wait_ge(s["rows_zero"], 16 * NS)

            def chunk_scatter(n, par):
                wait(pool, s["fence"], n)
                pool.wait_ge(s[f"rc{par}"], (n - par) * 24 + 48)
                nc.gpsimd.tensor_tensor(fence_p[:, 0:1], eps_col[:], eps_col[:], ALU.add).then_inc(s["fence"], 1)
                for k in range(2):
                    nc.gpsimd.indirect_dma_start(
                        xs_rows, bass.IndirectOffsetOnAxis(ap=row_chunk[par][:, k:k + 1], axis=0),
                        pair_chunk[par][:, k, :], None).then_inc(s[f"scat{par}"], 16)

            def step(i, par):
                if within(i, NT):
                    for g in (0, 2):
                        pool.wait_ge(s["s_h"], NB * i + g + 1)
                        wait(pool, s["y_psum"], i - 1)
                        nc.gpsimd.tensor_tensor(s_r[:, par, 1, g], s_f[:, g],
                                                s_r[:, par, 0, g].bitcast(F32), ALU.subtract).then_inc(s["s_l_pool"], 1)
                n, np_ = i + 1, 1 - par
                if within(n, NT):
                    pool.wait_ge(s["k_h"], n + 1)
                    nc.gpsimd.tensor_tensor(k_r[:, np_, 1], kq_f[:, np_, 0:D], k_r[:, np_, 0].bitcast(F32), ALU.subtract).then_inc(s["k_l"], 1)
                if within(i - 1, NT):
                    pool.wait_ge(s["st_h"], i)
                    nc.gpsimd.tensor_tensor(state_r[:, 1], state_f.rearrange("p c i -> p (c i)"),
                                            state_r[:, 0].bitcast(F32), ALU.subtract).then_inc(s["st_l"], 1)
                if within(i + 2, NT):
                    chunk_scatter(i + 2, par)

            run_steps(pool, -2, NT + 1, 4, 28, step)

            def slot_low(sl, par, k, cols):
                raw, parts_ = ((w1_raw, w1_r), (w2_raw, w2_r))[k]
                pool.wait_ge(s[f"w{k + 1}_h"], sl + 1)
                nc.gpsimd.tensor_tensor(parts_[:, par, 1, 0:cols], raw[:, par, 0:cols], parts_[:, par, 0, 0:cols].bitcast(F32),
                                        ALU.subtract).then_inc(s[f"w{k + 1}_l"], 1)

            def rows_scatter(sl, par):
                pool.wait_ge(s["ys_sb"], sl + 1)
                wait(pool, s["fence"], NT + sl)
                nc.gpsimd.tensor_tensor(fence_p[:, 0:1], eps_col[:], eps_col[:], ALU.add).then_inc(s["fence"], 1)
                for j in range(SJ):
                    nc.gpsimd.indirect_dma_start(
                        pair_rows, bass.IndirectOffsetOnAxis(ap=pair_slot[:, par, j, 0:1].bitcast(I32), axis=0),
                        ys[:, j * D:(j + 1) * D], None).then_inc(s["pairs_out"], 16)

            def slot_step(sl, par):
                if within(sl + 1, NS):
                    slot_low(sl + 1, 1 - par, 0, KC * F)
                if within(sl - 1, NS):
                    rows_scatter(sl - 1, 1 - par)
                if within(sl + 1, NS):
                    slot_low(sl + 1, 1 - par, 1, W2_POOL)

            slot_low(0, 0, 0, KC * F)
            slot_low(0, 0, 1, W2_POOL)
            run_steps(pool, 0, NS + 1, 2, NS - 1, slot_step)

            def pair_sum(hb, par):
                pool.wait_ge(s[f"pair_in{par}"], (hb - par) * 8 + 16)
                wait(pool, s["y_res"], hb - 1)
                nc.gpsimd.tensor_tensor(y_sum[:, par], y_pair[:, par, :, 0], y_pair[:, par, :, 1], ALU.add).then_inc(s["y_sum"], 1)

            run_steps(pool, 0, 2 * B, 2, 2 * B, pair_sum)

        @block.scalar
        def _(act):
            def ln_std(g, par):
                act.wait_ge(s["ln_var"], g + 1)
                nc.scalar.activation(std[:, par], mean_var[:, par, :, 1], ACT.Sqrt, bias=eps_col[:, 0:1]).then_inc(s["ln_std"], 1)

            def ln_copies(g, par):
                wait(act, s["ln_logit_psum"], g - 1)
                for k in range(KC):
                    act.wait_ge(s["ln_t_psum"], KC * g + k + 1)
                    nc.scalar.activation(x_grp_t[:, par, k], ps[:, 2 * par + k, :], ACT.Copy).then_inc(s["ln_t_sb"], 1)
                act.wait_ge(s["ln_xg"], g + 1)
                nc.scalar.activation(xn[:, bass.ds(g * GRP, GRP), :], x_grp[:, par], ACT.Copy).then_inc(s["ln_xn"], 1)

            def step(g, par):
                if within(g + 1, NG):
                    ln_std(g + 1, 1 - par)
                if within(g, NG):
                    ln_copies(g, par)

            act.wait_ge(s["tri_done"], 2)
            run_steps(act, -1, NG, 2, NG - 2, step)
            for n, (dst, name) in enumerate(((wq, "wq_in"), (wkv, "wkv_in"), (wo, "wo_in"))):
                act.wait_ge(s[name], 16)
                nc.scalar.activation(dst[:].rearrange("p s k n -> p s (k n)")[:, 0], w_raw[n], ACT.Copy).then_inc(s["w_split_h"], 1)
            act.wait_ge(s["route"], 1)
            nc.scalar.activation(rt[2], rt[1], ACT.Exp).then_inc(s["route_exp"], 1)

            def score_high(i, par, g):
                act.wait_ge(s["s_f"], NB * i + g + 1)
                wait(act, s["y_psum"], i - 1)
                nc.scalar.activation(s_r[:, par, 0, g], s_f[:, g], ACT.Copy).then_inc(s["s_h"], 1)

            def chunk(i, par):
                n, np_ = i + 1, 1 - par
                if within(n, NT):
                    act.wait_ge(s["kqt_psum"], n + 1)
                    wait(act, s["across_done"], n - 1)
                    nc.scalar.activation(kq_t[:, np_, :, 0], ps[:, 5, :].rearrange("p (w n) -> p w n", w=2), ACT.Copy).then_inc(s["kqt_h"], 1)
                if within(i, NT):
                    score_high(i, par, 0)
                    score_high(i, par, 1)
                if within(i + 2, NT):
                    m = i + 2
                    act.wait_ge(s["xt_psum"], m + 1)
                    wait(act, s["q_psum"], m - 1)
                    nc.scalar.activation(xt[:, par, 0], ps[:, 4, 0:256], ACT.Copy).then_inc(s["xt_h"], 1)
                if within(i, NT):
                    score_high(i, par, 2)
                    score_high(i, par, 3)
                if within(n, NT):
                    act.wait_ge(s["k_f"], n + 1)
                    wait(act, s["u_psum"], n - 1)
                    nc.scalar.activation(k_r[:, np_, 0], kq_f[:, np_, 0:D], ACT.Copy).then_inc(s["k_h"], 1)
                if within(i - 1, NT):
                    act.wait_ge(s["st_f"], i + 1)
                    act.wait_ge(s["across_done"], i)
                    nc.scalar.activation(state_r[:, 0], state_f.rearrange("p c i -> p (c i)"), ACT.Copy).then_inc(s["st_h"], 1)
                if within(n, NT):
                    act.wait_ge(s["v_f"], n + 1)
                    wait(act, s["y_psum"], n - 1)
                    nc.scalar.activation(v_r[:, np_, :, 0], v_f[:, np_].rearrange("p (h d) -> p h d", h=H), ACT.Copy).then_inc(s["v_h"], 1)
                if within(i - 2, NT):
                    m = i - 2
                    act.wait_ge(s["yt_psum"], m + 1)
                    nc.scalar.activation(y_t[:, bass.ds(m, 1)].rearrange("p a c i -> p (a c i)"), ps[:, 6, 0:256], ACT.Copy).then_inc(s["y_t"], 1)
                if within(i + 2, NT):
                    m = i + 2
                    act.wait_ge(s["k_f"], m + 1)
                    wait(act, s["v_l"], m - 1)
                    nc.scalar.activation(v_f[:, par], ps[:, 4, D:2 * D], ACT.Copy).then_inc(s["v_f"], 1)

            run_steps(act, -2, NT + 2, 4, 28, chunk)

            act.wait_ge(s["gn_var"], 1)
            nc.scalar.activation(gn_t[:, 5], gn_t[:, 4], ACT.Sqrt, bias=eps_col[:, 0:1]).then_inc(s["gn_std"], 1)

            def w_high(k, sl, par):
                raw, parts_ = ((w1_raw, w1_r), (w2_raw, w2_r))[k]
                act.wait_ge(s[f"w{k + 1}_in{par}"], (sl - par) * 8 + 16)
                wait(act, s["ys_psum"] if k else s["h_psum"], sl - 1 if k else FC // 2 * (sl - 1))
                nc.scalar.activation(parts_[:, par, 0], raw[:, par], ACT.Copy).then_inc(s[f"w{k + 1}_h"], 1)

            def xs_high(sl, par):
                act.wait_ge(s["xst_psum"], sl + 1)
                wait(act, s["h_psum"], FC // 2 * sl)
                nc.scalar.activation(xs_r[:, 0], ps[:, par, :], ACT.Copy).then_inc(s["xst_h"], 1)

            def slot_step(sl, par):
                if within(sl + 1, NS):
                    w_high(0, sl + 1, 1 - par)
                act.wait_ge(s[f"bias_in{par}"], (sl - par) * 16 + 32)
                for hp in range(FC // 2):
                    m = sl * (FC // 2) + hp
                    act.wait_ge(s["h_psum"], m + 1)
                    wait(act, s["h_l"], m - 1)
                    for o in range(2):
                        last = nc.scalar.activation(h_f[:, hp % 2, o * SLOT:(o + 1) * SLOT], ps[:, 2 + hp, o * SLOT:(o + 1) * SLOT], ACT.Relu,
                                                    bias=b1_slot[:, par, 2 * hp + o:2 * hp + o + 1])
                    last.then_inc(s["h_f"], 1)
                if within(sl + 1, NS):
                    xs_high(sl + 1, 1 - par)
                    w_high(1, sl + 1, 1 - par)

            w_high(0, 0, 0)
            xs_high(0, 0)
            w_high(1, 0, 0)
            run_steps(act, 0, NS, 2, NS - 1, slot_step)

            act.wait_ge(s["gn_ab"], 2)
            act.wait_ge(s["pairs_out"], 32 * NS)
            scale = gn_ab[:, 0].rearrange("p b h c -> p (b h) c")
            shift = gn_ab[:, 1].rearrange("p b h c -> p (b h) c")

            def norm_half(hb, par):
                wait(act, s["yn_l"], hb - 1)
                for c in range(KC):
                    nc.scalar.activation(yn_f[:, par, c].rearrange("p (t i) -> p t i", t=4), y_t[:, bass.ds(hb * 4, 4), c], ACT.Identity,
                                         scale=scale[:, bass.ds(hb, 1), c], bias=shift[:, bass.ds(hb, 1), c]).then_inc(s["yn_f"], 1)
                act.wait_ge(s["yn_f"], hb * 2 + 2)
                wait(act, s["o_psum"], hb - 1)
                nc.scalar.activation(yn_r[:, par, 0], yn_f[:, par], ACT.Copy).then_inc(s["yn_h"], 1)

            run_steps(act, 0, 2 * B, 2, 2 * B, norm_half)

        @block.tensor
        def _(pe):
            pe.wait_ge(s["consts_in"], 16)
            pe.wait_ge(s["small_in"], 48)

            def parts(out_ap, lhs, rhs, start, stop, **kw):
                for n, (a, b) in enumerate(PASSES):
                    last = pe.matmul(out_ap, lhs(a), rhs(b), start=start and n == 0, stop=stop and n == 2, **kw)
                return last

            def ln_transposes(g, par):
                pe.wait_ge(s["ln_xg"], g + 1)
                wait(pe, s["ln_t_sb"], KC * (g - 1))
                for k in range(KC):
                    for t in range(GRP):
                        last = pe.transpose(ps[:, 2 * par + k, t * P:(t + 1) * P], x_grp[:, par, t, k * P:(k + 1) * P], ident)
                    last.then_inc(s["ln_t_psum"], 1)

            def ln_logits(g, par):
                pe.wait_ge(s["ln_t_sb"], KC * (g + 1))
                wait(pe, s["ln_logit"], g - 1)
                for t in range(GRP):
                    for k in range(KC):
                        last = pe.matmul(ps[:, 4 + par, t * E:(t + 1) * E], x_grp_t[:, par, k, t * P:(t + 1) * P], gate_w[:, k, :],
                                         start=(k == 0), stop=(k == KC - 1))
                last.then_inc(s["ln_logit_psum"], 1)

            def ln_step(g, par):
                if within(g, NG):
                    ln_transposes(g, par)
                if within(g - 1, NG):
                    ln_logits(g - 1, 1 - par)

            run_steps(pe, 0, NG + 1, 4, NG, ln_step)

            def x_transposes(n, par):
                pe.wait_ge(s[f"xc{par}"], (n - par) * 8 + 16)
                wait(pe, s["v_f"], n)
                for k in range(KC):
                    last = pe.transpose(ps[:, 4, k * P:(k + 1) * P], x_chunk[par][:, k * P:(k + 1) * P], ident)
                last.then_inc(s["xt_psum"], 1)

            def projections(n, par):
                pe.wait_ge(s["xt_h"], n + 1)
                pe.wait_ge(s["xt_l"], n + 1)
                for m, (a, b) in enumerate(PASSES):
                    for k in range(KC):
                        last = pe.matmul(ps[:, 4, :], xt[:, par, a, k * P:(k + 1) * P], wkv[:, b, k, :],
                                         start=(m == 0 and k == 0), stop=(m == 2 and k == KC - 1))
                last.then_inc(s["kv_psum"], 1)
                wait(pe, s["kqt_h"], n)
                wait(pe, s["kqt_l"], n)
                for m, (a, b) in enumerate(PASSES):
                    for k in range(KC):
                        last = pe.matmul(ps[:, 5, 0:D], xt[:, par, a, k * P:(k + 1) * P], wq[:, b, k, :],
                                         start=(m == 0 and k == 0), stop=(m == 2 and k == KC - 1))
                last.then_inc(s["q_psum"], 1)

            def kq_transposes(n, par):
                pe.wait_ge(s["k_f"], n + 1)
                pe.wait_ge(s["q_f"], n + 1)
                for c in range(2 * KC):
                    last = pe.transpose(ps[:, 5, c * P:(c + 1) * P], kq_f[:, par, c * P:(c + 1) * P], ident)
                last.then_inc(s["kqt_psum"], 1)

            def scores(n, par):
                pe.wait_ge(s["kqt_h"], n + 1)
                pe.wait_ge(s["kqt_l"], n + 1)
                pe.wait_ge(s[f"q_diag{par}"], (n - par) * 64 + 128)
                for g in range(NB):
                    wait(pe, s["s_f"], NB * (n - 1) + g + 1 if not isinstance(n, int) or n > 0 else 0)
                    c, col = g // 2, g % 2 * HB * P
                    parts(ps[:, g, :], lambda a: kq_t[:, par, 0, a, c * P:(c + 1) * P],
                          lambda b: q_diag[:, par, b, c, col:col + HB * P], True, True).then_inc(s["s_psum"], 1)

            def across(n, par):
                wait(pe, s["st_h"], n)
                wait(pe, s["st_l"], n)
                wait(pe, s["y_f"], n)
                y_bank = ps[:, 7, :].rearrange("p (h s d) -> p h s d", h=H, s=2)
                for c in range(KC):
                    last = parts(y_bank[:, c * HP:(c + 1) * HP, 0], lambda a: kq_t[:, par, 1, a, c * P:(c + 1) * P],
                                 lambda b: state_r[:, b, c * P:(c + 1) * P], c == 0, False, skip_group_check=True)
                last.then_inc(s["across_done"], 1)

            def inside(n, par):
                pe.wait_ge(s["s_h"], NB * (n + 1))
                pe.wait_ge(s["s_l_pool"], 2 * (n + 1))
                pe.wait_ge(s["s_l_dve"], 2 * (n + 1))
                for h in range(H):
                    for a in range(2):
                        last = pe.matmul(ps[:, 7, h * 2 * DH:(h + 1) * 2 * DH],
                                         s_r[:, par, a, h // HB, h % HB * P:(h % HB + 1) * P],
                                         v_r[:, par, h].rearrange("p s d -> p (s d)"), start=False,
                                         stop=(h == H - 1 and a == 1), skip_group_check=True)
                last.then_inc(s["y_psum"], 1)

            def state_sums(n, par):
                pe.wait_ge(s["k_h"], n + 1)
                pe.wait_ge(s["k_l"], n + 1)
                pe.wait_ge(s["v_h"], n + 1)
                pe.wait_ge(s["v_l"], n + 1)
                wait(pe, s["y_t"], n - 1)
                for c in range(KC):
                    last = parts(ps[:, 6, 256 + c * P:256 + (c + 1) * P], lambda a: k_r[:, par, a, c * P:(c + 1) * P],
                                 lambda b: v_r[:, par, c * HP:(c + 1) * HP, b], c == 0, c == KC - 1, skip_group_check=True)
                last.then_inc(s["u_psum"], 1)

            def y_transposes(n, par):
                pe.wait_ge(s["y_f"], n + 1)
                wait(pe, s["y_t"], n)
                pe.wait_ge(s["st_t"], min(n + 2, NT) if isinstance(n, int) else n + 2)
                for c in range(KC):
                    last = pe.transpose(ps[:, 6, c * P:(c + 1) * P], y_f[:, par, c * P:(c + 1) * P], ident)
                last.then_inc(s["yt_psum"], 1)

            def chunk(i, par):
                if within(i + 1, NT):
                    kq_transposes(i + 1, 1 - par)
                if within(i, NT):
                    scores(i, par)
                if within(i + 2, NT):
                    x_transposes(i + 2, par)
                if within(i - 1, NT):
                    state_sums(i - 1, 1 - par)
                    inside(i - 1, 1 - par)
                if within(i - 2, NT):
                    y_transposes(i - 2, par)
                if within(i + 2, NT):
                    projections(i + 2, par)
                if within(i, NT):
                    across(i, par)

            pe.wait_ge(s["ln_logit"], NG)
            x_transposes(0, 0)
            pe.wait_ge(s["w_split_h"], 3)
            pe.wait_ge(s["w_split_l"], 3)
            projections(0, 0)
            pe.wait_ge(s["route_mask"], 1)
            pe.wait_ge(s["tri_done"], 3)
            for k in range(2):
                last = pe.matmul(ps[:, 6 + k, 0:NT * E], ident_bf[:, k], mask_bf[:], start=True, stop=True)
            last.then_inc(s["route_psum"], 1)
            chunk(-1, 1)
            pe.wait_ge(s["rows_done"], 2)
            pe.wait_ge(s["r_zero"], 3)
            run_steps(pe, 0, NT + 2, 4, 28, chunk)

            def slot_transposes(sl, par):
                pe.wait_ge(s[f"xs_in{par}"], (sl - par) * 8 + 16)
                wait(pe, s["xst_h"], sl - 1)
                wait(pe, s["xst_l"], sl - 1)
                for k in range(KC):
                    for j in range(SJ):
                        last = pe.transpose(ps[:, par, (k * SJ + j) * P:(k * SJ + j + 1) * P], xs[:, par, j, k * P:(k + 1) * P], ident)
                last.then_inc(s["xst_psum"], 1)

            def layer1(sl, par):
                pe.wait_ge(s["w1_h"], sl + 1)
                pe.wait_ge(s["w1_l"], sl + 1)
                pe.wait_ge(s["xst_h"], sl + 1)
                pe.wait_ge(s["xst_l"], sl + 1)
                for hp in range(FC // 2):
                    wait(pe, s["h_f"], (sl - 1) * (FC // 2) + hp + 1 if not isinstance(sl, int) or sl else 0)
                    for o in range(2):
                        for m, (a, b) in enumerate(PASSES):
                            for k in range(KC):
                                at = k * F + (2 * hp + o) * P
                                last = pe.matmul(ps[:, 2 + hp, o * SLOT:(o + 1) * SLOT], w1_r[:, par, a, at:at + P],
                                                 xs_r[:, b, k * SLOT:(k + 1) * SLOT],
                                                 start=(m == 0 and k == 0), stop=(m == 2 and k == KC - 1))
                    last.then_inc(s["h_psum"], 1)

            def layer2(sl, par):
                pe.wait_ge(s["w2_h"], sl + 1)
                pe.wait_ge(s["w2_l"], sl + 1)
                pe.wait_ge(s["w2_l_dve"], sl + 1)
                wait(pe, s["ys_sb"], sl - 1)
                for hc in range(FC):
                    if hc % 2 == 0:
                        pe.wait_ge(s["h_l"], sl * (FC // 2) + hc // 2 + 1)
                    for j in range(SJ):
                        at = hc * SLOT + j * P
                        last = parts(ps[:, 6 + par, j * D:(j + 1) * D], lambda a: h_r[:, a, at:at + P],
                                     lambda b: w2_r[:, par, b, hc * D:(hc + 1) * D], hc == 0 and j == 0, hc == FC - 1, skip_group_check=True)
                last.then_inc(s["ys_psum"], 1)

            def slot_step(sl, par):
                layer1(sl, par)
                if within(sl + 1, NS):
                    slot_transposes(sl + 1, 1 - par)
                layer2(sl, par)

            pe.wait_ge(s["y_t"], NT)
            pe.wait_ge(s["s_f"], NT * NB)
            pe.wait_ge(s["gn_chain"], 4)
            pe.matmul(ps[:, 7, 0:2 * B * KC], C["group_mean"], gn_t[:, 0:2].rearrange("p a b c -> p (a b c)"),
                      start=True, stop=True).then_inc(s["gn_avg_psum"], 1)
            slot_transposes(0, 0)
            run_steps(pe, 0, NS, 2, NS - 1, slot_step)

            pe.wait_ge(s["ys_sb"], NS)

            def out_half(hb, par):
                pe.wait_ge(s["yn_h"], hb + 1)
                pe.wait_ge(s["yn_l"], hb + 1)
                wait(pe, s["out_sb"], hb - 1)
                for t in range(4):
                    for m, (a, b) in enumerate(PASSES):
                        for k in range(KC):
                            last = pe.matmul(ps[:, par * 2 + t // 2, t % 2 * D:(t % 2 + 1) * D], yn_r[:, par, a, k, t * P:(t + 1) * P], wo[:, b, k, :],
                                             start=(m == 0 and k == 0 and t % 2 == 0), stop=(m == 2 and k == KC - 1), skip_group_check=True)
                last.then_inc(s["o_psum"], 1)

            run_steps(pe, 0, 2 * B, 2, 2 * B, out_half)

        @block.vector
        def _(dve):
            nc.vector.memset(eps_col[:], EPS).then_inc(s["tri_done"], 1)
            nc.vector.memset(ident_bf[:, 0], 1.0).then_inc(s["tri_done"], 1)

            def ln_stats(g, par):
                dve.wait_ge(s[f"x_in{g}"], 16)
                for t in range(GRP):
                    nc.vector.bn_stats(stats[:, par, t], xn[:, g * GRP + t]).then_inc(s["ln_stats"], 1)
                dve.wait_ge(s["ln_stats"], GRP * (g + 1))
                nc.vector.tensor_copy(fence_d[:, 0:1], eps_col[:])
                for t in range(GRP):
                    last = nc.vector.bn_aggr(mean_var[:, par, t], stats[:, par, t])
                last.then_inc(s["ln_var"], 1)

            def ln_norm(g, par):
                dve.wait_ge(s["ln_std"], g + 1)
                nc.vector.reciprocal(rstd[:, par], std[:, par]).then_inc(s["ln_rstd"], 1)
                dve.wait_ge(s["ln_rstd"], g + 1)
                wait(dve, s["ln_t_psum"], KC * (g - 1))
                wait(dve, s["ln_xn"], g - 1)
                for t in range(GRP):
                    last = nc.vector.tensor_scalar(x_grp[:, par, t], xn[:, g * GRP + t], mean_var[:, par, t, 0:1], rstd[:, par, t:t + 1],
                                                   ALU.subtract, ALU.mult)
                last.then_inc(s["ln_xg"], 1)

            def ln_logit(g, par):
                dve.wait_ge(s["small_in"], 48)
                dve.wait_ge(s["ln_logit_psum"], g + 1)
                nc.vector.tensor_tensor(logits[:, bass.ds(g * GRP, GRP), :], ps[:, 4 + par, 0:GRP * E].rearrange("p (t e) -> p t e", t=GRP),
                                        gate_bias[:].unsqueeze(1).to_broadcast([P, GRP, E]), ALU.add).then_inc(s["ln_logit"], 1)

            def ln_step(g, par):
                if within(g + 1, NG):
                    ln_stats(g + 1, 1 - par)
                if within(g, NG):
                    ln_norm(g, par)
                if within(g - 2, NG):
                    ln_logit(g - 2, par)

            for g in range(-1, NG + 2):
                ln_step(g, g % 2)

            dve.wait_ge(s["consts_in"], 16)
            nc.vector.tensor_tensor(ident_bf[:, 1], C["causal"], ident, ALU.subtract).then_inc(s["tri_done"], 1)
            count = [0]

            def chained(ins, n=1):
                count[0] += 1
                ins.then_inc(s["dve_route"], 1)
                dve.wait_ge(s["dve_route"], count[0])

            def over_e(a):
                return a.unsqueeze(2).to_broadcast([P, NT, E])

            def over_t(a):
                return a.unsqueeze(1).to_broadcast([P, NT, E])

            V = nc.vector
            rest, shifted, probs, first, second, tmp = rt
            peak, total, one = rs[:, 0], rs[:, 1], rs[:, 2]

            def first_of_max(onehot, scores_, peak_):
                chained(V.tensor_tensor(tmp, scores_, over_e(peak_), ALU.is_equal))
                chained(V.tensor_tensor(tmp, tmp, over_t(C["rank_low"]), ALU.mult))
                chained(V.tensor_reduce(one, tmp, AX, ALU.max))
                chained(V.tensor_tensor(onehot, tmp, over_e(one), ALU.is_equal))

            by_expert = rest.rearrange("p t e -> p (t e)").rearrange("p (e t) -> p e t", e=E)
            upto = shifted.rearrange("p t e -> p (t e)").rearrange("p (e t) -> p e t", e=E)
            tokens, slots, slot_end, base, ones_e, before = (re[:, i] for i in range(6))

            def first_expert():
                dve.wait_ge(s["ln_logit"], NG)
                chained(V.tensor_reduce(peak, logits[:], AX, ALU.max))
                V.tensor_tensor(shifted, logits[:], over_e(peak), ALU.subtract).then_inc(s["route"], 1)

                first_of_max(first, logits[:], peak)

            def second_expert():
                chained(V.scalar_tensor_tensor(rest, first, -BIG, logits[:], ALU.mult, ALU.add))
                chained(V.tensor_reduce(peak, rest, AX, ALU.max))
                first_of_max(second, rest, peak)
                chained(V.tensor_tensor(tmp, first, second, ALU.add))
                V.tensor_copy(mask_bf[:], tmp.rearrange("p t e -> p (t e)")).then_inc(s["route_mask"], 1)

            def gate_values():
                chained(V.tensor_copy(pair_info[:, :, :, 0].bitcast(I32), C["pair_no"].rearrange("p (t k) -> p t k", k=2)))
                dve.wait_ge(s["route_exp"], 1)
                chained(V.tensor_reduce(total, probs, AX, ALU.add))
                chained(V.reciprocal(total, total))
                chained(V.tensor_tensor(probs, probs, over_e(total), ALU.mult))
                for k, onehot in enumerate((first, second)):
                    chained(V.tensor_tensor(tmp, probs, onehot, ALU.mult))
                    chained(V.tensor_reduce(pair_info[:, :, k, 1], tmp, AX, ALU.add))

            def slots_of_experts():
                dve.wait_ge(s["route_psum"], 1)
                chained(V.tensor_copy(by_expert, ps[:, 6, 0:NT * E].rearrange("p (t e) -> p e t", t=NT)))
                chained(V.memset(tmp, 1.0))
                chained(V.tensor_tensor_scan(upto.rearrange("p e t -> p (e t)"), tmp.rearrange("p t e -> p (t e)"),
                                             by_expert.rearrange("p e t -> p (e t)"), 0.0, ALU.mult, ALU.add))
                last_t = upto[:, :, NT - 1]
                chained(V.memset(before[:, 0:1], 0.0))
                chained(V.tensor_copy(before[:, 1:E], last_t[:, 0:E - 1]))
                chained(V.tensor_tensor(tokens, last_t, before, ALU.subtract))
                chained(V.tensor_tensor(rk[:], tokens.unsqueeze(2).to_broadcast([P, E, NK]),
                                        C["slot_rows"].unsqueeze(1).to_broadcast([P, E, NK]), ALU.is_gt))
                chained(V.tensor_reduce(slots, rk[:], AX, ALU.add))
                chained(V.memset(ones_e, 1.0))
                chained(V.tensor_tensor_scan(slot_end, ones_e, slots, 0.0, ALU.mult, ALU.add))
                chained(V.tensor_tensor(base, slot_end, slots, ALU.subtract))
                chained(V.scalar_tensor_tensor(base, base, float(SLOT), before, ALU.mult, ALU.subtract))

            def rows_of_tokens():
                chained(V.tensor_tensor(upto, upto, by_expert, ALU.subtract))
                chained(V.tensor_tensor(upto, upto, base.unsqueeze(2).to_broadcast([P, E, NT]), ALU.add))
                chained(V.tensor_tensor(rest, ps[:, 7, 0:NT * E].rearrange("p (t e) -> p t e", t=NT),
                                        upto.rearrange("p e t -> p t e"), ALU.add))
                for k, onehot in enumerate((first, second)):
                    chained(V.tensor_tensor(tmp, rest, onehot, ALU.mult))
                    chained(V.tensor_reduce(rs[:, 4 + k], tmp, AX, ALU.add))
                    V.tensor_copy(rows2[:, :, k], rs[:, 4 + k]).then_inc(s["rows_done"], 1)

            def experts_of_slots():
                chained(V.tensor_tensor(rse, C["slot_no"].unsqueeze(2).to_broadcast([P, NS, E]),
                                        slot_end.unsqueeze(1).to_broadcast([P, NS, E]), ALU.is_ge))
                chained(V.tensor_reduce(slot_expert[:], rse, AX, ALU.add))
                chained(V.tensor_scalar(slot_expert[:], slot_expert[:], float(E - 1), None, ALU.min))
                V.tensor_copy(expert_of[:], slot_expert[:]).then_inc(s["route_done"], 1)

            def tokens_low(m, par):
                dve.wait_ge(s["xt_h"], m + 1)
                wait(dve, s["q_psum"], m - 1)
                V.tensor_tensor(xt[:, par, 1], ps[:, 4, 0:256], xt[:, par, 0].bitcast(F32), ALU.subtract).then_inc(s["xt_l"], 1)

            def keys_and_queries(m, par):
                dve.wait_ge(s["kv_psum"], m + 1)
                wait(dve, s["k_l"], m - 1)
                wait(dve, s["kqt_psum"], m - 1)
                V.tensor_tensor(kq_f[:, par, 0:D], ps[:, 4, 0:D], C["tab_k"], ALU.mult).then_inc(s["k_f"], 1)
                dve.wait_ge(s["q_psum"], m + 1)
                V.tensor_tensor(kq_f[:, par, D:2 * D], ps[:, 5, 0:D], C["tab_q"], ALU.mult).then_inc(s["q_f"], 1)

            def transposed_low(n, par):
                dve.wait_ge(s["kqt_h"], n + 1)
                wait(dve, s["across_done"], n - 1)
                V.tensor_tensor(kq_t[:, par, :, 1], ps[:, 5, :].rearrange("p (w n) -> p w n", w=2),
                                kq_t[:, par, :, 0].bitcast(F32), ALU.subtract).then_inc(s["kqt_l"], 1)

            def values_low(n, par):
                dve.wait_ge(s["v_h"], n + 1)
                V.tensor_tensor(v_r[:, par, :, 1], v_f[:, par].rearrange("p (h d) -> p h d", h=H),
                                v_r[:, par, :, 0].bitcast(F32), ALU.subtract).then_inc(s["v_l"], 1)

            def score_low(i, par, g):
                dve.wait_ge(s["s_h"], NB * i + g + 1)
                wait(dve, s["y_psum"], i - 1)
                V.tensor_tensor(s_r[:, par, 1, g], s_f[:, g], s_r[:, par, 0, g].bitcast(F32), ALU.subtract).then_inc(s["s_l_dve"], 1)

            def masked_scores(i, g):
                dve.wait_ge(s["s_psum"], NB * i + g + 1)
                if g % 2 == 0:
                    wait(dve, s["s_l_pool"], 2 * (i - 1) + g // 2 + 1 if not isinstance(i, int) or i > 0 else 0)
                V.tensor_tensor(s_f[:, g].rearrange("p (h i) -> p h i", h=HB), ps[:, g, :].rearrange("p (h i) -> p h i", h=HB),
                                C["causal"].unsqueeze(1).to_broadcast([P, HB, P]), ALU.mult).then_inc(s["s_f"], 1)

            def new_state(m):
                dve.wait_ge(s["u_psum"], m + 1)
                dve.wait_ge(s["st_f"], m + 1)
                V.tensor_tensor(state_t, ps[:, 6, 256:512].rearrange("p (c i) -> p c i", c=KC), state_f, ALU.add).then_inc(s["st_t"], 1)
                dve.wait_ge(s["st_t"], m + 1)
                wait(dve, s["st_h"], m)
                wait(dve, s["st_l"], m)
                V.scalar_tensor_tensor(state_f, state_t, C["keep"][:, bass.ds(m + 1, 1)], decay, ALU.mult, ALU.mult).then_inc(s["st_f"], 1)

            def output_stats(m):
                dve.wait_ge(s["y_t"], m + 1)
                for c in range(KC):
                    V.bn_stats(y_stats[:, c, bass.ds(m, 1)].rearrange("p a k -> p (a k)"),
                               y_t[:, bass.ds(m, 1), c].rearrange("p a i -> p (a i)")).then_inc(s["y_stats"], 1)

            def output_sum(m, par):
                dve.wait_ge(s["y_psum"], m + 1)
                wait(dve, s["yt_psum"], m - 1)
                V.tensor_reduce(y_f[:, par].rearrange("p (h d) -> p h d", h=H),
                                ps[:, 7, :].rearrange("p (h s d) -> p h d s", h=H, s=2), AX, ALU.add).then_inc(s["y_f"], 1)

            def chunk(i, par):
                if within(i + 1, NT):
                    transposed_low(i + 1, 1 - par)
                if within(i, NT):
                    for g in range(NB):
                        masked_scores(i, g)
                if within(i + 2, NT):
                    tokens_low(i + 2, par)
                if within(i, NT):
                    score_low(i, par, 1)
                if within(i - 1, NT):
                    new_state(i - 1)
                if within(i, NT):
                    score_low(i, par, 3)
                if within(i - 3, NT):
                    output_stats(i - 3)
                if within(i - 1, NT):
                    output_sum(i - 1, 1 - par)
                if within(i + 1, NT):
                    values_low(i + 1, 1 - par)
                if within(i + 2, NT):
                    keys_and_queries(i + 2, par)

            first_expert()
            tokens_low(0, 0)
            second_expert()
            gate_values()
            keys_and_queries(0, 0)
            slots_of_experts()
            transposed_low(0, 0)
            tokens_low(1, 1)
            rows_of_tokens()
            values_low(0, 0)
            keys_and_queries(1, 1)
            experts_of_slots()
            dve.wait_ge(s["ln_xn"], NG)
            V.memset(state_f, 0.0).then_inc(s["st_f"], 1)
            run_steps(dve, 0, NT + 3, 4, 28, chunk)

            gn_count = [0]

            def gn(ins):
                gn_count[0] += 1
                ins.then_inc(s["gn_chain"], 1)
                dve.wait_ge(s["gn_chain"], gn_count[0])

            dve.wait_ge(s["y_stats"], KC * NT)
            for b in range(B):
                for c in range(KC):
                    last = V.bn_aggr(y_mv[:, b, c], y_stats[:, c, b * CB:(b + 1) * CB].rearrange("p a b -> p (a b)"))
            gn(last)
            mean, square, head_mean, head_square, var, std_, scale_t, shift_t = (gn_t[:, k] for k in range(8))
            gn(V.tensor_tensor(square, y_mv[:, :, :, 0], y_mv[:, :, :, 0], ALU.mult))
            V.tensor_copy(mean, y_mv[:, :, :, 0]).then_inc(s["gn_chain"], 1)
            V.tensor_tensor(square, square, y_mv[:, :, :, 1], ALU.add).then_inc(s["gn_chain"], 1)
            gn_count[0] += 2
            dve.wait_ge(s["gn_avg_psum"], 1)
            gn(V.tensor_copy(gn_t[:, 2:4].rearrange("p a b c -> p (a b c)"), ps[:, 7, 0:2 * B * KC]))
            gn(V.tensor_tensor(var, head_mean, head_mean, ALU.mult))
            V.tensor_tensor(var, head_square, var, ALU.subtract).then_inc(s["gn_var"], 1)
            dve.wait_ge(s["gn_std"], 1)
            gn(V.reciprocal(std_, std_))
            gn(V.tensor_tensor(scale_t, std_, gn_sb[:, 0].unsqueeze(1).to_broadcast([P, B, KC]), ALU.mult))
            gn(V.tensor_tensor(shift_t, head_mean, scale_t, ALU.mult))
            gn(V.tensor_tensor(shift_t, gn_sb[:, 1].unsqueeze(1).to_broadcast([P, B, KC]), shift_t, ALU.subtract))
            for k, src in enumerate((scale_t, shift_t)):
                V.tensor_copy(gn_ab[:, k], src.unsqueeze(2).to_broadcast([P, B, 2, KC])).then_inc(s["gn_ab"], 1)

            def xs_low(sl, par):
                dve.wait_ge(s["xst_h"], sl + 1)
                wait(dve, s["h_psum"], FC // 2 * sl)
                V.tensor_tensor(xs_r[:, 1], ps[:, par, :], xs_r[:, 0].bitcast(F32), ALU.subtract).then_inc(s["xst_l"], 1)

            def ys_gated(sl, par):
                dve.wait_ge(s["ys_psum"], sl + 1)
                dve.wait_ge(s[f"bias_in{par}"], (sl - par) * 16 + 32)
                wait(dve, s["pairs_out"], 32 * sl)
                V.tensor_tensor(ys.rearrange("p (j d) -> p j d", j=SJ), ps[:, 6 + par, :].rearrange("p (j d) -> p j d", j=SJ),
                                b2_slot[:, par].unsqueeze(1).to_broadcast([P, SJ, D]), ALU.add).then_inc(s["ys_sum"], 1)
                dve.wait_ge(s["ys_sum"], sl + 1)
                dve.wait_ge(s[f"pair_slot{par}"], (sl - par) * 8 + 16)
                for j in range(SJ):
                    last = V.tensor_scalar(ys[:, j * D:(j + 1) * D], ys[:, j * D:(j + 1) * D], pair_slot[:, par, j, 1:2], None, ALU.mult)
                last.then_inc(s["ys_sb"], 1)

            def w2_low(sl, par):
                dve.wait_ge(s["w2_h"], sl + 1)
                V.tensor_tensor(w2_r[:, par, 1, W2_POOL:FC * D], w2_raw[:, par, W2_POOL:FC * D], w2_r[:, par, 0, W2_POOL:FC * D].bitcast(F32),
                                ALU.subtract).then_inc(s["w2_l_dve"], 1)

            def slot_step(sl, par):
                for hp in range(FC // 2):
                    m = sl * (FC // 2) + hp
                    cols = slice(hp * 2 * SLOT, (hp + 1) * 2 * SLOT)
                    dve.wait_ge(s["h_f"], m + 1)
                    wait(dve, s["ys_psum"], sl)
                    V.tensor_copy(h_r[:, 0, cols], h_f[:, hp % 2]).then_inc(s["h_h"], 1)
                    if hp == 0 and within(sl - 1, NS):
                        ys_gated(sl - 1, 1 - par)
                    dve.wait_ge(s["h_h"], m + 1)
                    V.tensor_tensor(h_r[:, 1, cols], h_f[:, hp % 2], h_r[:, 0, cols].bitcast(F32), ALU.subtract).then_inc(s["h_l"], 1)
                if within(sl + 1, NS):
                    xs_low(sl + 1, 1 - par)
                    w2_low(sl + 1, 1 - par)

            xs_low(0, 0)
            w2_low(0, 0)
            run_steps(dve, 0, NS, 2, NS - 1, slot_step)
            ys_gated(NS - 1, (NS - 1) % 2)

            dve.wait_ge(s["pairs_out"], 32 * NS)

            def low_half(hb, par):
                dve.wait_ge(s["yn_h"], hb + 1)
                wait(dve, s["o_psum"], hb - 1)
                V.tensor_tensor(yn_r[:, par, 1], yn_f[:, par], yn_r[:, par, 0].bitcast(F32), ALU.subtract).then_inc(s["yn_l"], 1)

            def out_half(hb, par):
                if within(hb + 1, 2 * B):
                    low_half(hb + 1, 1 - par)
                dve.wait_ge(s[f"x_res_in{par}"], (hb - par) * 8 + 16)
                dve.wait_ge(s["y_sum"], hb + 1)
                wait(dve, s[f"out_done{par}"], (hb - par) * 8)
                V.tensor_tensor(out_sb[:, par], y_sum[:, par], x_res[:, par], ALU.add).then_inc(s["y_res"], 1)
                dve.wait_ge(s["y_res"], hb + 1)
                dve.wait_ge(s["o_psum"], hb + 1)
                V.tensor_tensor(out_sb[:, par].rearrange("p t d -> p (t d)"), ps[:, par * 2:par * 2 + 2, :].rearrange("p a b -> p (a b)"),
                                out_sb[:, par].rearrange("p t d -> p (t d)"), ALU.add).then_inc(s["out_sb"], 1)

            low_half(0, 0)
            run_steps(dve, 0, 2 * B, 2, 2 * B - 2, out_half)


def kernel(L0_attn_x, L0_attn_W_q, L0_attn_W_k, L0_attn_W_v, L0_attn_W_o, L0_attn_gn_weight, L0_attn_gn_bias,
           L0_ffn_gate_w, L0_ffn_gate_b, L0_ffn_w1, L0_ffn_b1, L0_ffn_w2, L0_ffn_b2):
    import concourse.bacc as bacc
    from concourse.bass_utils import run_bass_kernel_spmd

    const, where = constants()
    a = np.asarray
    gn = np.stack([a(L0_attn_gn_weight).reshape(KC, P), a(L0_attn_gn_bias).reshape(KC, P)]).transpose(2, 0, 1)
    arrays = {
        "x": a(L0_attn_x),
        "wq_t": a(L0_attn_W_q).T,
        "wkv_t": np.concatenate([a(L0_attn_W_k).T, a(L0_attn_W_v).T], 1),
        "wo_t": a(L0_attn_W_o).T,
        "gn": gn,
        "gate_t": a(L0_ffn_gate_w).T,
        "gate_b": a(L0_ffn_gate_b),
        "w1": a(L0_ffn_w1).reshape(E, KC, P, F).transpose(0, 2, 1, 3).reshape(E, P, KC * F),
        "w2": a(L0_ffn_w2).reshape(E, FC, P, D).transpose(0, 2, 1, 3).reshape(E, P, FC * D),
        "b1": a(L0_ffn_b1).reshape(E, FC, P).transpose(0, 2, 1),
        "b2": a(L0_ffn_b2),
        "const": const,
    }
    arrays = {k: np.ascontiguousarray(v) for k, v in arrays.items()}
    nc = bacc.Bacc("TRN2", target_bir_lowering=False, num_devices=1)
    args = {k: nc.dram_tensor(k, v.shape, mybir.dt.from_np(v.dtype), kind="ExternalInput").ap() for k, v in arrays.items()}
    out = nc.dram_tensor("out", (B, T, D), F32, kind="ExternalOutput").ap()
    build(nc, where, out=out, **args)
    r = run_bass_kernel_spmd(nc, [arrays], core_ids=[0])
    return r.results[0]["out"]
```

```python
from contextlib import ExitStack

import numpy as np

import concourse.bass as bass
from concourse import mybir

F32 = mybir.dt.float32
FR = mybir.dt.float32r
BF16 = mybir.dt.bfloat16
I32 = mybir.dt.int32
ALU = mybir.AluOpType
ACT = mybir.ActivationFunctionType
AX = mybir.AxisListType.X

P = 128
B, T, D = 4, 1024, 256
KC = D // P
NT = B * T // P
CB = T // P
H, DH = 16, 16
HP = P // DH
HB = 4
NB = H // HB
E, F = 8, 1024
FC = F // P
SLOT = 256
SJ = SLOT // P
NS = (2 * NT * P - E) // SLOT + E
NK = NT * P // SLOT
EPS = 1e-5
GRP = 4
NG = NT // GRP
BIG = 1e30
W2_POOL = 1280
W = D + 2

PASSES = ((0, 0), (0, 1), (1, 0))


def constants():
    i = np.arange(P)
    gam = 1.0 - 2.0 ** (-5.0 - np.arange(H, dtype=np.float64))
    head = (np.arange(D) // DH)
    local = (i % P) // DH
    tab_q = gam[head][None, :] ** (i[:, None] - 64.0) / np.sqrt(DH)
    same = local[:, None] == local[None, :]
    decay = np.stack([same * (gam[c * HP + local] ** P)[:, None] for c in range(KC)], 1)
    keep = np.ones((P, NT + 1))
    keep[:, ::CB] = 0.0
    cols = {
        "ident": np.eye(P),
        "causal": (i[None, :] >= i[:, None]) * 1.0,
        "tab_q": tab_q,
        "tab_k": gam[head][None, :] ** (64.0 - i[:, None]),
        "decay": decay.reshape(P, -1),
        "group_mean": same / DH,
        "keep": keep,
        "slot_rows": np.tile(np.arange(NK) * float(SLOT), (P, 1)),
        "slot_no": np.tile(np.arange(NS) * 1.0, (P, 1)),
        "pair_no": (np.arange(NT)[None, :, None] * P + i[:, None, None]).repeat(2, 2).reshape(P, -1) * 2.0
        + np.tile([0.0, 1.0], NT),
        "spare_no": 2.0 * NT * P + i[:, None] * SJ + np.arange(SJ)[None, :],
        "rank_low": np.tile(E - np.arange(E) * 1.0, (P, 1)),
    }
    at, where = 0, {}
    for name, a in cols.items():
        where[name] = (at, at + a.shape[1])
        at += a.shape[1]
    return np.concatenate(list(cols.values()), 1).astype(np.float32), where


def run_steps(eng, first, last, lo, hi, step):
    for i in range(first, lo):
        step(i, i % 2)
    assert lo % 2 == 0 and hi % 2 == 0
    with eng.Fori(lo // 2, hi // 2) as pair:
        step(pair * 2, 0)
        step(pair * 2 + 1, 1)
    for i in range(hi, last):
        step(i, i % 2)


def within(n, count):
    return not isinstance(n, int) or 0 <= n < count


def wait(eng, sem, value):
    if isinstance(value, int) and value <= 0:
        return
    eng.wait_ge(sem, value)


def build(nc, where, x, wq_t, wkv_t, wo_t, gn, gate_t, gate_b, w1, w2, b1, b2, const, out):
    xs_rows = nc.dram_tensor("xs_rows", [NS * SLOT, W], F32).ap()
    pair_rows = nc.dram_tensor("pair_rows", [2 * NT * P + SLOT, D], F32).ap()
    pair_tiles = pair_rows[0:2 * NT * P].rearrange("(t p k) d -> p t (k d)", p=P, k=2)
    x_tiles = x.rearrange("b (c p) d -> p (b c) d", p=P)
    out_tiles = out.rearrange("b (c p) d -> p (b c) d", p=P)
    xs_slots = xs_rows.rearrange("(s p j) d -> s p (j d)", p=P, j=SJ)

    with ExitStack() as ctx:
        def sb(name, shape, dt=F32):
            return ctx.enter_context(nc.sbuf_tensor(name, shape, dt))

        def sem(name):
            return ctx.enter_context(nc.semaphore(name))

        class Arena:

            def __init__(self, name, words, dt):
                self.t, self.words, self.at = sb(name, [P, words], dt), words, 0

            def __call__(self, *dims):
                n = int(np.prod(dims))
                a = self.t[:, self.at:self.at + n]
                self.at += n
                assert self.at <= self.words, (self.at, self.words)
                names = "abcd"[:len(dims)]
                if len(dims) > 1:
                    a = a.rearrange(f"p ({' '.join(names)}) -> p {' '.join(names)}",
                                    **{k: v for k, v in zip(names, dims)})
                return a

        cst = sb("cst", [P, const.shape[1]])
        C = {k: cst[:, a:b] for k, (a, b) in where.items()}
        ident = C["ident"]
        decay = C["decay"].rearrange("p (c i) -> p c i", c=KC)
        xn = sb("xn", [P, NT, D])
        y_t = xn[:].rearrange("p t (c i) -> p t c i", c=KC)
        wq = sb("wq", [P, 2, KC, D], FR)
        wkv = sb("wkv", [P, 2, KC, 2 * D], FR)
        wo = sb("wo", [P, 2, KC, D], FR)
        gn_sb = sb("gn_sb", [P, 2, KC])
        gate_w = sb("gate_w", [P, KC, E])
        gate_bias = sb("gate_bias", [P, E])
        pair_info = sb("pair_info", [P, NT, 2, 2])
        rows2 = sb("rows2", [P, NT, 2], I32)
        expert_of = sb("expert_of", [P, NS], I32)
        logits = sb("logits", [P, NT, E])
        token_sets = sb("token_sets", [P, 2, P], BF16)
        mask_bf = sb("mask_bf", [P, NT * E], BF16)
        eps_col = sb("eps_col", [P, 1])
        fence_out = sb("fence_out", [P, 1])
        spare_rows = sb("spare_rows", [P, SJ, W])

        fr = Arena("arena_r", 22016, FR)
        ff = Arena("arena_f", 12352, F32)

        w_raw = [ff(KC * cols) for cols in (D, 2 * D, D)]
        x_grp = ff(2, GRP, D)
        x_grp_t = ff(2, KC, GRP * P)
        logit_t = sb("logit_t", [E, 2, GRP * P])
        stats = sb("stats", [P, 2, GRP, 6])
        mean_var = sb("mean_var", [P, 2, GRP, 2])
        std = sb("std", [P, 2, GRP])
        rstd = sb("rstd", [P, 2, GRP])
        rt = [ff(NT, E) for _ in range(6)]
        rs = sb("rs", [P, 6, NT])
        slot_expert = sb("slot_expert", [P, NS])
        re = sb("re", [P, 6, E])
        rk = sb("rk", [P, E, NK])
        rse = ff(NS, E)
        ff.at = 0
        x_chunk = [sb(f"x_chunk{i}", [P, D]) for i in range(2)]
        pair_chunk = [sb(f"pair_chunk{i}", [P, 2, W]) for i in range(2)]
        row_chunk = [sb(f"row_chunk{i}", [P, 2], I32) for i in range(2)]
        kq_f = ff(2, 2 * D)
        v_f = ff(2, D)
        s_f = ff(NB, HB * P)
        y_f = ff(2, D)
        state_f = ff(KC, P)
        state_t = ff(KC, P)
        xt = fr(2, 2, KC * P)
        k_r = fr(2, 2, D)
        v_r = fr(2, H, 2, DH)
        kq_t = fr(2, 2, 2, KC * P)
        diag_at = fr.at
        q_diag = fr(2, 2, KC, HP * P)
        s_r = fr(2, 2, NB, HB * P)
        state_r = fr(2, KC * P)
        y_stats = sb("y_stats", [P, KC, NT, 6])
        after_f = ff.at
        xs = ff(2, SJ, W)
        b1_slot = ff(2, FC)
        b2_slot = ff(2, D)
        gate_slot = ff(2, SJ)
        raw_at = ff.at
        w1_raw, w2_raw = [ff(KC * F), None], [ff(FC * D), None]
        w2_raw[1] = ff(FC * D)
        pair_slot = sb("pair_slot", [P, 2, SJ], I32)
        ff.at = 0
        w1_raw[1] = ff(KC * F)
        h_f = ff(2, 2 * SLOT)
        ys = ff(SJ * D)
        assert ff.at <= after_f
        fr.at = 0
        xs_r = fr(2, KC * SLOT)
        h_r = fr(2, FC * SLOT)
        assert fr.at <= diag_at
        fr.at = diag_at
        w1_r, w2_r = [fr(2, KC * F), None], [fr(2, FC * D), None]
        w1_r[1], w2_r[1] = fr(2, KC * F), fr(2, FC * D)
        ff.at = raw_at
        x_res = [ff(CB, D) for b in range(B - 1)]
        ff.at = 0
        x_res.append(ff(CB, D))
        y_pair = ff(4, 2, 2, D)
        assert ff.at <= raw_at
        fr.at = 0
        yn_r = fr(2, 2, KC, 4 * P)

        def x_rows(tile, count):
            return x_res[tile // CB][:, tile % CB:tile % CB + count]

        y_mv = sb("y_mv", [P, B, KC, 2])
        gn_t = sb("gn_t", [P, 8, B, KC])
        gn_ab = sb("gn_ab", [P, 2, B, 2, KC])

        ps = ctx.enter_context(nc.psum_tensor("ps", [P, 8, 512], F32))

        s = {}
        for name in (
            "consts_in gn_in wq_in wkv_in wo_in small_in w_split_h w_split_l zeroed spare_rows_out "
            "x_in0 x_in1 x_in2 x_in3 x_in4 x_in5 x_in6 x_in7 "
            "ln_stats ln_var ln_std ln_rstd ln_xg ln_t_psum ln_t_sb ln_logit_psum ln_logit_t ln_back_psum ln_logit ln_xn "
            "route dve_route route_exp route_mask route_psum rows_done route_done tables_done "
            "xc0 xc1 rc0 rc1 xt_psum xt_h xt_l kv_psum q_psum k_f k_h k_l v_f v_h v_l q_f kqt_psum kqt_h kqt_l q_diag0 q_diag1 "
            "s_psum s_f s_h s_l_pool s_l_dve y_psum across_done u_psum st_t st_f st_h st_l y_f yt_psum y_t y_stats "
            "fence scat0 scat1 r_zero "
            "gn_chain gn_avg_psum gn_var gn_std gn_ab yn_f yn_h yn_l o_psum x_res_in0 x_res_in1 x_res_in2 x_res_in3 "
            "xs_in0 xs_in1 bias_in0 bias_in1 w1_in0 w1_in1 w2_in0 w2_in1 w1_h w1_l w2_h w2_l xst_psum xst_h xst_l "
            "h_psum h_f h_h h_l ys_psum ys_sum ys_sb pair_slot w2_l_dve pairs_out spare y_sum attn_res out_sb out_done "
            "pair_in0 pair_in1 pair_in2 pair_in3"
        ).split():
            s[name] = sem(name)

        block = ctx.enter_context(nc.Block())

        @block.sync
        def _(sp):
            def ln_load(g):
                tiles = slice(g * GRP, (g + 1) * GRP)
                sp.dma_start(xn[:, tiles, :], x_tiles[:, tiles, :]).then_inc(s[f"x_in{g}"], 16)

            ln_load(0)
            sp.dma_start(cst[:], const).then_inc(s["consts_in"], 16)
            sp.dma_start(gate_w[:], gate_t.rearrange("(k p) e -> p k e", p=P)).then_inc(s["small_in"], 16)
            sp.dma_start(gate_bias[:], gate_b.rearrange("(a e) -> a e", a=1).to_broadcast([P, E])).then_inc(s["small_in"], 16)
            for g in range(1, NG):
                ln_load(g)
            sp.dma_start(gn_sb[:], gn).then_inc(s["gn_in"], 16)
            for k, (src, name) in enumerate(((wq_t, "wq_in"), (wkv_t, "wkv_in"), (wo_t, "wo_in"))):
                sp.dma_start(w_raw[k].rearrange("p (k n) -> p k n", k=KC),
                             src.rearrange("(k p) n -> p k n", p=P)).then_inc(s[name], 16)

            def tokens_stage(n, par):
                sp.dma_start(x_chunk[par][:], xn[:, bass.ds(n, 1), :].rearrange("p a d -> p (a d)")).then_inc(s[f"xc{par}"], 16)

            def pairs_stage(n, par):
                sp.dma_start(pair_chunk[par][:, :, 0:D], xn[:, bass.ds(n, 1), :].to_broadcast([P, 2, D])).then_inc(s[f"rc{par}"], 16)
                sp.dma_start(pair_chunk[par][:, :, D:W], pair_info[:, bass.ds(n, 1)].rearrange("p a k w -> p (a k) w")).then_inc(s[f"rc{par}"], 16)
                sp.dma_start(row_chunk[par][:], rows2[:, bass.ds(n, 1), :].rearrange("p a d -> p (a d)")).then_inc(s[f"rc{par}"], 16)

            def queries_to_diagonal(n, par):
                wait(sp, s["s_psum"], NB * (n - 1))
                sp.wait_ge(s["kqt_h"], n + 1)
                sp.wait_ge(s["kqt_l"], n + 1)
                for h in range(HP):
                    r = slice(h * DH, (h + 1) * DH)
                    sp.dma_start(q_diag[r, par, :, :, h * P:(h + 1) * P].bitcast(F32).rearrange("p s c i -> p (s c) i"),
                                 kq_t[r, par, 1].bitcast(F32).rearrange("p s (c i) -> p (s c) i", c=KC)).then_inc(s[f"q_diag{par}"], 16)

            sp.wait_ge(s["ln_xn"], 1)
            tokens_stage(0, 0)
            tokens_stage(1, 1)
            sp.wait_ge(s["spare"], 1)
            with sp.Fori(0, NS) as sl:
                sp.dma_start(xs_slots[bass.ds(sl, 1)].rearrange("a p d -> (a p) d"),
                             spare_rows[:].rearrange("p j d -> p (j d)")).then_inc(s["spare_rows_out"], 16)
            sp.wait_ge(s["r_zero"], 3)
            queries_to_diagonal(0, 0)
            sp.wait_ge(s["rows_done"], 2)
            pairs_stage(0, 0)
            pairs_stage(1, 1)
            sp.wait_ge(s["ln_xn"], NG)
            sp.wait_ge(s["xt_psum"], 1)
            tokens_stage(2, 0)

            def chunk_step(i, par):
                if within(i + 3, NT):
                    wait(sp, s["xt_psum"], i + 2)
                    tokens_stage(i + 3, 1 - par)
                if within(i + 1, NT):
                    queries_to_diagonal(i + 1, 1 - par)
                if within(i + 2, NT):
                    wait(sp, s[f"scat{par}"], (i - par) * 16 + 32)
                    pairs_stage(i + 2, par)

            run_steps(sp, 0, NT, 4, 28, chunk_step)

            sp.wait_ge(s["route_done"], 1)
            for par in range(2):
                sp.wait_ge(s[f"scat{par}"], 16 * NT)

            def expert(sl):
                return bass.ds(sp.value_load(expert_of[0:1, bass.ds(sl, 1)], min_val=0, max_val=E - 1), 1)

            def slot_load(sl, par):
                e = expert(sl)
                wait(sp, s["w1_h"], sl - 1)
                wait(sp, s["w1_l"], sl - 1)
                sp.dma_start(w1_raw[par], w1[e].rearrange("a p n -> (a p) n")).then_inc(s[f"w1_in{par}"], 16)
                wait(sp, s["w2_h"], sl - 1)
                wait(sp, s["w2_l"], sl - 1)
                wait(sp, s["w2_l_dve"], sl - 1)
                sp.dma_start(w2_raw[par], w2[e].rearrange("a p n -> (a p) n")).then_inc(s[f"w2_in{par}"], 16)
                wait(sp, s["xst_psum"], sl - 1)
                wait(sp, s["pair_slot"], sl - 1)
                sp.dma_start(xs[:, par].rearrange("p j d -> p (j d)"),
                             xs_slots[bass.ds(sl, 1)].rearrange("a p d -> (a p) d")).then_inc(s[f"xs_in{par}"], 16)

            def bias_load(sl, par):
                e = expert(sl)
                wait(sp, s["ys_sb"], sl - 1)
                sp.dma_start(b1_slot[:, par], b1[e].rearrange("a p n -> (a p) n")).then_inc(s[f"bias_in{par}"], 16)
                sp.dma_start(b2_slot[:, par], b2[e].to_broadcast([P, D])).then_inc(s[f"bias_in{par}"], 16)

            slot_load(0, 0)
            bias_load(0, 0)
            sp.wait_ge(s["s_l_pool"], NB // 2 * NT)
            sp.wait_ge(s["s_l_dve"], NB // 2 * NT)
            slot_load(1, 1)

            def slot_step(sl, par):
                if within(sl + 2, NS):
                    slot_load(sl + 2, par)
                if within(sl + 1, NS):
                    bias_load(sl + 1, 1 - par)

            def tokens_load(b, slots):
                for name in ("w1_h", "w1_l", "w2_h", "w2_l", "w2_l_dve"):
                    sp.wait_ge(s[name], slots)
                sp.dma_start(x_res[b], x_tiles[:, b * CB:(b + 1) * CB, :]).then_inc(s[f"x_res_in{b}"], 16)

            run_steps(sp, 0, NS - 2, 2, NS - 3, slot_step)
            tokens_load(3, NS - 1)
            tokens_load(2, NS - 1)
            slot_step(NS - 2, NS % 2)
            tokens_load(0, NS)
            tokens_load(1, NS)

            def pair_rows_load(q):
                sp.dma_start(y_pair[:, q % 4].rearrange("p t k d -> p t (k d)"),
                             pair_tiles[:, q * 2:q * 2 + 2, :]).then_inc(s[f"pair_in{q % 4}"], 16)

            sp.wait_ge(s["pairs_out"], 32 * NS)
            for q in range(4):
                pair_rows_load(q)
            for q in range(NT // 2):
                sp.wait_ge(s["out_sb"], q + 1)
                if q + 4 < NT // 2:
                    pair_rows_load(q + 4)
                sp.dma_start(out_tiles[:, q * 2:q * 2 + 2, :], x_rows(q * 2, 2)).then_inc(s["out_done"], 16)
            sp.wait_ge(s["out_done"], 16 * NT // 2)
            sp.wait_ge(s["spare_rows_out"], 16 * NS)

        @block.gpsimd
        def _(pool):
            nc.gpsimd.memset(spare_rows[:], 0.0).then_inc(s["zeroed"], 1)
            nc.gpsimd.memset(state_r.bitcast(F32), 0.0).then_inc(s["r_zero"], 1)
            for par in range(2):
                nc.gpsimd.memset(q_diag[:, par].bitcast(F32), 0.0).then_inc(s["r_zero"], 1)
            pool.wait_ge(s["consts_in"], 16)
            pool.wait_ge(s["zeroed"], 1)
            nc.gpsimd.tensor_copy(spare_rows[:, :, D:D + 1], C["spare_no"].unsqueeze(2)).then_inc(s["spare"], 1)
            for n, dst in enumerate((wq, wkv, wo)):
                pool.wait_ge(s["w_split_h"], n + 1)
                flat = dst[:].rearrange("p s k n -> p s (k n)")
                nc.gpsimd.tensor_tensor(flat[:, 1], w_raw[n], flat[:, 0].bitcast(F32), ALU.subtract).then_inc(s["w_split_l"], 1)
            pool.wait_ge(s["spare_rows_out"], 16 * NS)

            def chunk_scatter(n, par):
                wait(pool, s["fence"], n)
                pool.wait_ge(s[f"rc{par}"], (n - par) * 24 + 48)
                nc.gpsimd.tensor_tensor(fence_out[:, 0:1], eps_col[:], eps_col[:], ALU.add).then_inc(s["fence"], 1)
                for k in range(2):
                    nc.gpsimd.indirect_dma_start(
                        xs_rows, bass.IndirectOffsetOnAxis(ap=row_chunk[par][:, k:k + 1], axis=0),
                        pair_chunk[par][:, k, :], None).then_inc(s[f"scat{par}"], 16)

            def step(i, par):
                if within(i, NT):
                    for g in (0, 2):
                        pool.wait_ge(s["s_h"], NB * i + g + 1)
                        wait(pool, s["y_psum"], i - 1)
                        nc.gpsimd.tensor_tensor(s_r[:, par, 1, g], s_f[:, g],
                                                s_r[:, par, 0, g].bitcast(F32), ALU.subtract).then_inc(s["s_l_pool"], 1)
                n, np_ = i + 1, 1 - par
                if within(n, NT):
                    pool.wait_ge(s["k_h"], n + 1)
                    nc.gpsimd.tensor_tensor(k_r[:, np_, 1], kq_f[:, np_, 0:D], k_r[:, np_, 0].bitcast(F32), ALU.subtract).then_inc(s["k_l"], 1)
                if within(i - 1, NT):
                    pool.wait_ge(s["st_h"], i)
                    nc.gpsimd.tensor_tensor(state_r[:, 1], state_f.rearrange("p c i -> p (c i)"),
                                            state_r[:, 0].bitcast(F32), ALU.subtract).then_inc(s["st_l"], 1)
                if within(i + 2, NT):
                    chunk_scatter(i + 2, par)

            run_steps(pool, -2, NT, 4, 28, step)

            def slot_low(sl, par, k, cols):
                raw, parts_ = ((w1_raw, w1_r), (w2_raw, w2_r))[k]
                pool.wait_ge(s[f"w{k + 1}_h"], sl + 1)
                nc.gpsimd.tensor_tensor(parts_[par][:, 1, 0:cols], raw[par][:, 0:cols], parts_[par][:, 0, 0:cols].bitcast(F32),
                                        ALU.subtract).then_inc(s[f"w{k + 1}_l"], 1)

            def rows_scatter(sl, par):
                pool.wait_ge(s["ys_sb"], sl + 1)
                wait(pool, s["fence"], NT + sl)
                nc.gpsimd.tensor_tensor(fence_out[:, 0:1], eps_col[:], eps_col[:], ALU.add).then_inc(s["fence"], 1)
                for j in range(SJ):
                    nc.gpsimd.indirect_dma_start(
                        pair_rows, bass.IndirectOffsetOnAxis(ap=pair_slot[:, par, j:j + 1], axis=0),
                        ys[:, j * D:(j + 1) * D], None).then_inc(s["pairs_out"], 16)

            def slot_step(sl, par):
                if within(sl + 1, NS):
                    slot_low(sl + 1, 1 - par, 0, KC * F)
                if within(sl - 1, NS):
                    rows_scatter(sl - 1, 1 - par)
                if within(sl + 1, NS):
                    slot_low(sl + 1, 1 - par, 1, W2_POOL)

            slot_low(0, 0, 0, KC * F)
            step(NT, NT % 2)
            slot_low(0, 0, 1, W2_POOL)
            run_steps(pool, 0, NS + 1, 2, NS - 1, slot_step)

            for q in range(NT // 2):
                pool.wait_ge(s[f"pair_in{q % 4}"], q // 4 * 16 + 16)
                nc.gpsimd.tensor_tensor(y_pair[:, q % 4, :, 0], y_pair[:, q % 4, :, 0], y_pair[:, q % 4, :, 1], ALU.add).then_inc(s["y_sum"], 1)

        @block.scalar
        def _(act):
            def ln_std(g, par):
                act.wait_ge(s["ln_var"], g + 1)
                nc.scalar.activation(std[:, par], mean_var[:, par, :, 1], ACT.Sqrt, bias=eps_col[:, 0:1]).then_inc(s["ln_std"], 1)

            def ln_copies(g, par):
                wait(act, s["ln_logit_psum"], g - 1)
                for k in range(KC):
                    act.wait_ge(s["ln_t_psum"], KC * g + k + 1)
                    nc.scalar.activation(x_grp_t[:, par, k], ps[:, 2 * par + k, :], ACT.Copy).then_inc(s["ln_t_sb"], 1)
                act.wait_ge(s["ln_xg"], g + 1)
                nc.scalar.activation(xn[:, bass.ds(g * GRP, GRP), :], x_grp[:, par], ACT.Copy).then_inc(s["ln_xn"], 1)

            def ln_logit_copy(g, par):
                act.wait_ge(s["ln_logit_psum"], g + 1)
                wait(act, s["ln_back_psum"], g - 1)
                nc.scalar.activation(logit_t[:, par], ps[0:E, 4 + par, :], ACT.Copy).then_inc(s["ln_logit_t"], 1)

            def step(g, par):
                if within(g + 1, NG):
                    ln_std(g + 1, 1 - par)
                if within(g, NG):
                    ln_copies(g, par)
                if within(g - 1, NG):
                    ln_logit_copy(g - 1, 1 - par)

            def proj_weight_high(n):
                dst, name = ((wq, "wq_in"), (wkv, "wkv_in"), (wo, "wo_in"))[n]
                act.wait_ge(s[name], 16)
                nc.scalar.activation(dst[:].rearrange("p s k n -> p s (k n)")[:, 0], w_raw[n], ACT.Copy).then_inc(s["w_split_h"], 1)

            for g in range(-1, NG + 1):
                step(g, g % 2)
                if g >= NG - 3 and g < NG:
                    proj_weight_high(g - (NG - 3))

            def w_high(k, sl, par):
                raw, parts_ = ((w1_raw, w1_r), (w2_raw, w2_r))[k]
                act.wait_ge(s[f"w{k + 1}_in{par}"], (sl - par) * 8 + 16)
                wait(act, s["ys_psum"] if k else s["h_psum"], sl - 1 if k else FC // 2 * (sl - 1))
                nc.scalar.activation(parts_[par][:, 0], raw[par], ACT.Copy).then_inc(s[f"w{k + 1}_h"], 1)

            def score_high(i, par, g):
                act.wait_ge(s["s_f"], NB * i + g + 1)
                wait(act, s["y_psum"], i - 1)
                nc.scalar.activation(s_r[:, par, 0, g], s_f[:, g], ACT.Copy).then_inc(s["s_h"], 1)

            def chunk(i, par):
                n, np_ = i + 1, 1 - par
                if within(n, NT):
                    act.wait_ge(s["kqt_psum"], n + 1)
                    wait(act, s["across_done"], n - 1)
                    nc.scalar.activation(kq_t[:, np_, :, 0], ps[:, 5, :].rearrange("p (w n) -> p w n", w=2), ACT.Copy).then_inc(s["kqt_h"], 1)
                if within(i, NT):
                    score_high(i, par, 0)
                    score_high(i, par, 1)
                if within(i + 2, NT):
                    m = i + 2
                    act.wait_ge(s["xt_psum"], m + 1)
                    wait(act, s["q_psum"], m - 1)
                    nc.scalar.activation(xt[:, par, 0], ps[:, 4, 0:256], ACT.Copy).then_inc(s["xt_h"], 1)
                if within(i, NT):
                    score_high(i, par, 2)
                    score_high(i, par, 3)
                if isinstance(i, int) and i == -2:
                    act.wait_ge(s["route"], 1)
                    nc.scalar.activation(rt[2], rt[1], ACT.Exp).then_inc(s["route_exp"], 1)
                if isinstance(i, int) and i == NT - 1:
                    w_high(0, 0, 0)
                if within(n, NT):
                    act.wait_ge(s["k_f"], n + 1)
                    wait(act, s["u_psum"], n - 1)
                    nc.scalar.activation(k_r[:, np_, 0], kq_f[:, np_, 0:D], ACT.Copy).then_inc(s["k_h"], 1)
                if within(i - 1, NT):
                    act.wait_ge(s["st_f"], i + 1)
                    act.wait_ge(s["across_done"], i)
                    nc.scalar.activation(state_r[:, 0], state_f.rearrange("p c i -> p (c i)"), ACT.Copy).then_inc(s["st_h"], 1)
                if within(n, NT):
                    act.wait_ge(s["v_f"], n + 1)
                    wait(act, s["y_psum"], n - 1)
                    nc.scalar.activation(v_r[:, np_, :, 0], v_f[:, np_].rearrange("p (h d) -> p h d", h=H), ACT.Copy).then_inc(s["v_h"], 1)
                if within(i - 2, NT):
                    m = i - 2
                    act.wait_ge(s["yt_psum"], m + 1)
                    nc.scalar.activation(y_t[:, bass.ds(m, 1)].rearrange("p a c i -> p (a c i)"), ps[:, 6, 0:256], ACT.Copy).then_inc(s["y_t"], 1)
                if within(i + 2, NT):
                    m = i + 2
                    act.wait_ge(s["k_f"], m + 1)
                    wait(act, s["v_l"], m - 1)
                    nc.scalar.activation(v_f[:, par], ps[:, 4, D:2 * D], ACT.Copy).then_inc(s["v_f"], 1)

            run_steps(act, -2, NT, 4, 28, chunk)

            def xs_high(sl, par):
                act.wait_ge(s["xst_psum"], sl + 1)
                wait(act, s["h_psum"], FC // 2 * sl)
                nc.scalar.activation(xs_r[:, 0], ps[:, par, :], ACT.Copy).then_inc(s["xst_h"], 1)

            def slot_step(sl, par):
                if within(sl + 1, NS):
                    w_high(0, sl + 1, 1 - par)
                act.wait_ge(s[f"bias_in{par}"], (sl - par) * 16 + 32)
                for hp in range(FC // 2):
                    m = sl * (FC // 2) + hp
                    act.wait_ge(s["h_psum"], m + 1)
                    wait(act, s["h_l"], m - 1)
                    for o in range(2):
                        last = nc.scalar.activation(h_f[:, hp % 2, o * SLOT:(o + 1) * SLOT], ps[:, 2 + hp, o * SLOT:(o + 1) * SLOT], ACT.Relu,
                                                    bias=b1_slot[:, par, 2 * hp + o:2 * hp + o + 1])
                    last.then_inc(s["h_f"], 1)
                    if hp == 1 and within(sl + 1, NS):
                        w_high(1, sl + 1, 1 - par)
                if within(sl + 1, NS):
                    xs_high(sl + 1, 1 - par)

            w_high(1, 0, 0)
            xs_high(0, 0)
            chunk(NT, NT % 2)
            chunk(NT + 1, 1 - NT % 2)
            act.wait_ge(s["st_l"], NT)
            slot_step(0, 0)
            slot_step(1, 1)
            act.wait_ge(s["gn_var"], 1)
            nc.scalar.activation(gn_t[:, 5], gn_t[:, 4], ACT.Sqrt, bias=eps_col[:, 0:1]).then_inc(s["gn_std"], 1)
            run_steps(act, 2, NS, 2, NS - 1, slot_step)

            act.wait_ge(s["gn_ab"], 2)
            act.wait_ge(s["ys_psum"], NS)
            scale = gn_ab[:, 0].rearrange("p b h c -> p (b h) c")
            shift = gn_ab[:, 1].rearrange("p b h c -> p (b h) c")

            def norm_half(hb, par):
                for c in range(KC):
                    nc.scalar.activation(y_t[:, hb * 4:hb * 4 + 4, c], y_t[:, hb * 4:hb * 4 + 4, c], ACT.Identity,
                                         scale=scale[:, hb:hb + 1, c], bias=shift[:, hb:hb + 1, c]).then_inc(s["yn_f"], 1)
                act.wait_ge(s["yn_f"], hb * 2 + 2)
                wait(act, s["o_psum"], hb - 1)
                nc.scalar.activation(yn_r[:, par, 0].rearrange("p c (t i) -> p t c i", t=4), y_t[:, hb * 4:hb * 4 + 4],
                                     ACT.Copy).then_inc(s["yn_h"], 1)

            for hb in range(2 * B):
                norm_half(hb, hb % 2)

        @block.tensor
        def _(pe):
            pe.wait_ge(s["consts_in"], 16)
            pe.wait_ge(s["small_in"], 32)

            def parts(out_ap, lhs, rhs, start, stop, **kw):
                for n, (a, b) in enumerate(PASSES):
                    last = pe.matmul(out_ap, lhs(a), rhs(b), start=start and n == 0, stop=stop and n == 2, **kw)
                return last

            def ln_transposes(g, par):
                pe.wait_ge(s["ln_xg"], g + 1)
                wait(pe, s["ln_t_sb"], KC * (g - 1))
                for k in range(KC):
                    for t in range(GRP):
                        last = pe.transpose(ps[:, 2 * par + k, t * P:(t + 1) * P], x_grp[:, par, t, k * P:(k + 1) * P], ident)
                    last.then_inc(s["ln_t_psum"], 1)

            def ln_logits(g, par):
                pe.wait_ge(s["ln_t_sb"], KC * (g + 1))
                wait(pe, s["ln_logit_t"], g - 1)
                for k in range(KC):
                    last = pe.matmul(ps[0:E, 4 + par, :], gate_w[:, k, :], x_grp_t[:, par, k, :], start=(k == 0), stop=(k == KC - 1))
                last.then_inc(s["ln_logit_psum"], 1)

            def ln_back(g, par):
                pe.wait_ge(s["ln_logit_t"], g + 1)
                wait(pe, s["ln_logit"], g - 1)
                for t in range(GRP):
                    last = pe.transpose(ps[:, 6 + par, t * E:(t + 1) * E], logit_t[:, par, t * P:(t + 1) * P], ident[0:E, 0:E])
                last.then_inc(s["ln_back_psum"], 1)

            def ln_step(g, par):
                if within(g, NG):
                    ln_transposes(g, par)
                if within(g - 1, NG):
                    ln_logits(g - 1, 1 - par)
                if within(g - 2, NG):
                    ln_back(g - 2, par)

            for g in range(NG + 2):
                ln_step(g, g % 2)

            def x_transposes(n, par):
                pe.wait_ge(s[f"xc{par}"], (n - par) * 8 + 16)
                wait(pe, s["v_f"], n)
                for k in range(KC):
                    last = pe.transpose(ps[:, 4, k * P:(k + 1) * P], x_chunk[par][:, k * P:(k + 1) * P], ident)
                last.then_inc(s["xt_psum"], 1)

            def projections(n, par):
                pe.wait_ge(s["xt_h"], n + 1)
                pe.wait_ge(s["xt_l"], n + 1)
                for m, (a, b) in enumerate(PASSES):
                    for k in range(KC):
                        last = pe.matmul(ps[:, 4, :], xt[:, par, a, k * P:(k + 1) * P], wkv[:, b, k, :],
                                         start=(m == 0 and k == 0), stop=(m == 2 and k == KC - 1))
                last.then_inc(s["kv_psum"], 1)
                wait(pe, s["kqt_h"], n)
                wait(pe, s["kqt_l"], n)
                for m, (a, b) in enumerate(PASSES):
                    for k in range(KC):
                        last = pe.matmul(ps[:, 5, 0:D], xt[:, par, a, k * P:(k + 1) * P], wq[:, b, k, :],
                                         start=(m == 0 and k == 0), stop=(m == 2 and k == KC - 1))
                last.then_inc(s["q_psum"], 1)

            def kq_transposes(n, par):
                pe.wait_ge(s["k_f"], n + 1)
                pe.wait_ge(s["q_f"], n + 1)
                for c in range(2 * KC):
                    last = pe.transpose(ps[:, 5, c * P:(c + 1) * P], kq_f[:, par, c * P:(c + 1) * P], ident)
                last.then_inc(s["kqt_psum"], 1)

            def scores(n, par):
                pe.wait_ge(s["kqt_h"], n + 1)
                pe.wait_ge(s["kqt_l"], n + 1)
                pe.wait_ge(s[f"q_diag{par}"], (n - par) * 64 + 128)
                for g in range(NB):
                    wait(pe, s["s_f"], NB * (n - 1) + g + 1 if not isinstance(n, int) or n > 0 else 0)
                    c, col = g // 2, g % 2 * HB * P
                    parts(ps[:, g, :], lambda a: kq_t[:, par, 0, a, c * P:(c + 1) * P],
                          lambda b: q_diag[:, par, b, c, col:col + HB * P], True, True).then_inc(s["s_psum"], 1)

            def across(n, par):
                wait(pe, s["st_h"], n)
                wait(pe, s["st_l"], n)
                wait(pe, s["y_f"], n)
                y_bank = ps[:, 7, :].rearrange("p (h s d) -> p h s d", h=H, s=2)
                for c in range(KC):
                    last = parts(y_bank[:, c * HP:(c + 1) * HP, 0], lambda a: kq_t[:, par, 1, a, c * P:(c + 1) * P],
                                 lambda b: state_r[:, b, c * P:(c + 1) * P], c == 0, False, skip_group_check=True)
                last.then_inc(s["across_done"], 1)

            def inside(n, par):
                pe.wait_ge(s["s_h"], NB * (n + 1))
                pe.wait_ge(s["s_l_pool"], 2 * (n + 1))
                pe.wait_ge(s["s_l_dve"], 2 * (n + 1))
                for h in range(H):
                    for a in range(2):
                        last = pe.matmul(ps[:, 7, h * 2 * DH:(h + 1) * 2 * DH],
                                         s_r[:, par, a, h // HB, h % HB * P:(h % HB + 1) * P],
                                         v_r[:, par, h].rearrange("p s d -> p (s d)"), start=False,
                                         stop=(h == H - 1 and a == 1), skip_group_check=True)
                last.then_inc(s["y_psum"], 1)

            def state_sums(n, par):
                pe.wait_ge(s["k_h"], n + 1)
                pe.wait_ge(s["k_l"], n + 1)
                pe.wait_ge(s["v_h"], n + 1)
                pe.wait_ge(s["v_l"], n + 1)
                wait(pe, s["y_t"], n - 1)
                for c in range(KC):
                    last = parts(ps[:, 6, 256 + c * P:256 + (c + 1) * P], lambda a: k_r[:, par, a, c * P:(c + 1) * P],
                                 lambda b: v_r[:, par, c * HP:(c + 1) * HP, b], c == 0, c == KC - 1, skip_group_check=True)
                last.then_inc(s["u_psum"], 1)

            def y_transposes(n, par):
                pe.wait_ge(s["y_f"], n + 1)
                wait(pe, s["y_t"], n)
                pe.wait_ge(s["st_t"], min(n + 2, NT) if isinstance(n, int) else n + 2)
                for c in range(KC):
                    last = pe.transpose(ps[:, 6, c * P:(c + 1) * P], y_f[:, par, c * P:(c + 1) * P], ident)
                last.then_inc(s["yt_psum"], 1)

            def chunk(i, par):
                if within(i + 1, NT):
                    kq_transposes(i + 1, 1 - par)
                if within(i, NT):
                    scores(i, par)
                if within(i + 2, NT):
                    x_transposes(i + 2, par)
                if within(i - 1, NT):
                    state_sums(i - 1, 1 - par)
                    inside(i - 1, 1 - par)
                if within(i - 2, NT):
                    y_transposes(i - 2, par)
                if within(i + 2, NT):
                    projections(i + 2, par)
                if within(i, NT):
                    across(i, par)

            pe.wait_ge(s["ln_logit"], NG)
            x_transposes(0, 0)
            pe.wait_ge(s["w_split_h"], 3)
            pe.wait_ge(s["w_split_l"], 3)
            projections(0, 0)
            pe.wait_ge(s["route_mask"], 1)
            pe.wait_ge(s["tables_done"], 3)
            for k in range(2):
                last = pe.matmul(ps[:, 6 + k, 0:NT * E], token_sets[:, k], mask_bf[:], start=True, stop=True)
            last.then_inc(s["route_psum"], 1)
            chunk(-1, 1)
            pe.wait_ge(s["rows_done"], 2)
            pe.wait_ge(s["r_zero"], 3)
            run_steps(pe, 0, NT, 4, 28, chunk)

            def slot_transposes(sl, par):
                pe.wait_ge(s[f"xs_in{par}"], (sl - par) * 8 + 16)
                wait(pe, s["xst_h"], sl - 1)
                wait(pe, s["xst_l"], sl - 1)
                for k in range(KC):
                    for j in range(SJ):
                        last = pe.transpose(ps[:, par, (k * SJ + j) * P:(k * SJ + j + 1) * P], xs[:, par, j, k * P:(k + 1) * P], ident)
                last.then_inc(s["xst_psum"], 1)

            def layer1(sl, par):
                pe.wait_ge(s["w1_h"], sl + 1)
                pe.wait_ge(s["w1_l"], sl + 1)
                pe.wait_ge(s["xst_h"], sl + 1)
                pe.wait_ge(s["xst_l"], sl + 1)
                for hp in range(FC // 2):
                    wait(pe, s["h_f"], (sl - 1) * (FC // 2) + hp + 1 if not isinstance(sl, int) or sl else 0)
                    for o in range(2):
                        for m, (a, b) in enumerate(PASSES):
                            for k in range(KC):
                                at = k * F + (2 * hp + o) * P
                                last = pe.matmul(ps[:, 2 + hp, o * SLOT:(o + 1) * SLOT], w1_r[par][:, a, at:at + P],
                                                 xs_r[:, b, k * SLOT:(k + 1) * SLOT],
                                                 start=(m == 0 and k == 0), stop=(m == 2 and k == KC - 1))
                    last.then_inc(s["h_psum"], 1)

            def layer2(sl, par):
                pe.wait_ge(s["w2_h"], sl + 1)
                pe.wait_ge(s["w2_l"], sl + 1)
                pe.wait_ge(s["w2_l_dve"], sl + 1)
                wait(pe, s["ys_sb"], sl - 1)
                for hc in range(FC):
                    if hc % 2 == 0:
                        pe.wait_ge(s["h_l"], sl * (FC // 2) + hc // 2 + 1)
                    for j in range(SJ):
                        at = hc * SLOT + j * P
                        last = parts(ps[:, 6 + par, j * D:(j + 1) * D], lambda a: h_r[:, a, at:at + P],
                                     lambda b: w2_r[par][:, b, hc * D:(hc + 1) * D], hc == 0 and j == 0, hc == FC - 1, skip_group_check=True)
                last.then_inc(s["ys_psum"], 1)

            def slot_step(sl, par):
                layer1(sl, par)
                if within(sl + 1, NS):
                    slot_transposes(sl + 1, 1 - par)
                layer2(sl, par)

            pe.wait_ge(s["s_f"], NT * NB)
            slot_transposes(0, 0)
            chunk(NT, NT % 2)
            chunk(NT + 1, 1 - NT % 2)
            slot_step(0, 0)
            slot_step(1, 1)
            pe.wait_ge(s["gn_chain"], 4)
            pe.wait_ge(s["ys_sb"], 1)
            pe.matmul(ps[:, 6, 0:2 * B * KC], C["group_mean"], gn_t[:, 0:2].rearrange("p a b c -> p (a b c)"),
                      start=True, stop=True).then_inc(s["gn_avg_psum"], 1)
            pe.wait_ge(s["gn_chain"], 5)
            run_steps(pe, 2, NS, 2, NS - 1, slot_step)

            pe.wait_ge(s["ys_sb"], NS)

            def out_half(hb, par):
                pe.wait_ge(s["yn_h"], hb + 1)
                pe.wait_ge(s["yn_l"], hb + 1)
                wait(pe, s["attn_res"], hb - 1)
                for t in range(4):
                    for m, (a, b) in enumerate(PASSES):
                        for k in range(KC):
                            last = pe.matmul(ps[:, par * 2 + t // 2, t % 2 * D:(t % 2 + 1) * D], yn_r[:, par, a, k, t * P:(t + 1) * P], wo[:, b, k, :],
                                             start=(m == 0 and k == 0 and t % 2 == 0), stop=(m == 2 and k == KC - 1), skip_group_check=True)
                last.then_inc(s["o_psum"], 1)

            run_steps(pe, 0, 2 * B, 2, 2 * B, out_half)

        @block.vector
        def _(dve):
            nc.vector.memset(eps_col[:], EPS).then_inc(s["tables_done"], 1)
            nc.vector.memset(token_sets[:, 0], 1.0).then_inc(s["tables_done"], 1)

            def ln_stats(g, par):
                dve.wait_ge(s[f"x_in{g}"], 16)
                for t in range(GRP):
                    nc.vector.bn_stats(stats[:, par, t], xn[:, g * GRP + t]).then_inc(s["ln_stats"], 1)
                dve.wait_ge(s["ln_stats"], GRP * (g + 1))
                for t in range(GRP):
                    last = nc.vector.bn_aggr(mean_var[:, par, t], stats[:, par, t])
                last.then_inc(s["ln_var"], 1)

            def ln_norm(g, par):
                dve.wait_ge(s["ln_std"], g + 1)
                nc.vector.reciprocal(rstd[:, par], std[:, par]).then_inc(s["ln_rstd"], 1)
                dve.wait_ge(s["ln_rstd"], g + 1)
                wait(dve, s["ln_t_psum"], KC * (g - 1))
                wait(dve, s["ln_xn"], g - 1)
                for t in range(GRP):
                    last = nc.vector.tensor_scalar(x_grp[:, par, t], xn[:, g * GRP + t], mean_var[:, par, t, 0:1], rstd[:, par, t:t + 1],
                                                   ALU.subtract, ALU.mult)
                last.then_inc(s["ln_xg"], 1)

            def ln_logit(g, par):
                dve.wait_ge(s["small_in"], 32)
                dve.wait_ge(s["ln_back_psum"], g + 1)
                nc.vector.tensor_tensor(logits[:, bass.ds(g * GRP, GRP), :], ps[:, 6 + par, 0:GRP * E].rearrange("p (t e) -> p t e", t=GRP),
                                        gate_bias[:].unsqueeze(1).to_broadcast([P, GRP, E]), ALU.add).then_inc(s["ln_logit"], 1)

            def ln_step(g, par):
                if within(g + 1, NG):
                    ln_stats(g + 1, 1 - par)
                if within(g, NG):
                    ln_norm(g, par)
                if within(g - 3, NG):
                    ln_logit(g - 3, 1 - par)

            for g in range(-1, NG + 3):
                ln_step(g, g % 2)

            dve.wait_ge(s["consts_in"], 16)
            nc.vector.tensor_tensor(token_sets[:, 1], C["causal"], ident, ALU.subtract).then_inc(s["tables_done"], 1)
            count = [0]

            def chained(ins):
                count[0] += 1
                ins.then_inc(s["dve_route"], 1)
                dve.wait_ge(s["dve_route"], count[0])

            def over_e(a):
                return a.unsqueeze(2).to_broadcast([P, NT, E])

            def over_t(a):
                return a.unsqueeze(1).to_broadcast([P, NT, E])

            V = nc.vector
            rest, shifted, probs, first, second, tmp = rt
            peak, total, one = rs[:, 0], rs[:, 1], rs[:, 2]

            def first_of_max(onehot, scores_, peak_):
                chained(V.tensor_tensor(tmp, scores_, over_e(peak_), ALU.is_equal))
                chained(V.tensor_tensor(tmp, tmp, over_t(C["rank_low"]), ALU.mult))
                chained(V.tensor_reduce(one, tmp, AX, ALU.max))
                chained(V.tensor_tensor(onehot, tmp, over_e(one), ALU.is_equal))

            by_expert = rest.rearrange("p t e -> p (t e)").rearrange("p (e t) -> p e t", e=E)
            upto = shifted.rearrange("p t e -> p (t e)").rearrange("p (e t) -> p e t", e=E)
            tokens, slots, slot_end, base, ones_e, before = (re[:, i] for i in range(6))

            def shifted_logits():
                dve.wait_ge(s["ln_logit"], NG)
                chained(V.tensor_reduce(peak, logits[:], AX, ALU.max))
                V.tensor_tensor(shifted, logits[:], over_e(peak), ALU.subtract).then_inc(s["route"], 1)

            def first_expert():
                first_of_max(first, logits[:], peak)

            def second_expert():
                chained(V.scalar_tensor_tensor(rest, first, -BIG, logits[:], ALU.mult, ALU.add))
                chained(V.tensor_reduce(peak, rest, AX, ALU.max))
                first_of_max(second, rest, peak)
                chained(V.tensor_tensor(tmp, first, second, ALU.add))
                V.tensor_copy(mask_bf[:], tmp.rearrange("p t e -> p (t e)")).then_inc(s["route_mask"], 1)

            def gate_values():
                chained(V.tensor_copy(pair_info[:, :, :, 0], C["pair_no"].rearrange("p (t k) -> p t k", k=2)))
                dve.wait_ge(s["route_exp"], 1)
                chained(V.tensor_reduce(total, probs, AX, ALU.add))
                chained(V.reciprocal(total, total))
                chained(V.tensor_tensor(probs, probs, over_e(total), ALU.mult))
                for k, onehot in enumerate((first, second)):
                    chained(V.tensor_tensor(tmp, probs, onehot, ALU.mult))
                    chained(V.tensor_reduce(pair_info[:, :, k, 1], tmp, AX, ALU.add))

            def slots_of_experts():
                dve.wait_ge(s["route_psum"], 1)
                dve.wait_ge(s["route_exp"], 1)
                chained(V.tensor_copy(by_expert, ps[:, 6, 0:NT * E].rearrange("p (t e) -> p e t", t=NT)))
                chained(V.memset(tmp, 1.0))
                chained(V.tensor_tensor_scan(upto.rearrange("p e t -> p (e t)"), tmp.rearrange("p t e -> p (t e)"),
                                             by_expert.rearrange("p e t -> p (e t)"), 0.0, ALU.mult, ALU.add))
                last_t = upto[:, :, NT - 1]
                chained(V.memset(before[:, 0:1], 0.0))
                chained(V.tensor_copy(before[:, 1:E], last_t[:, 0:E - 1]))
                chained(V.tensor_tensor(tokens, last_t, before, ALU.subtract))
                chained(V.tensor_tensor(rk[:], tokens.unsqueeze(2).to_broadcast([P, E, NK]),
                                        C["slot_rows"].unsqueeze(1).to_broadcast([P, E, NK]), ALU.is_gt))
                chained(V.tensor_reduce(slots, rk[:], AX, ALU.add))
                chained(V.memset(ones_e, 1.0))
                chained(V.tensor_tensor_scan(slot_end, ones_e, slots, 0.0, ALU.mult, ALU.add))
                chained(V.tensor_tensor(base, slot_end, slots, ALU.subtract))
                chained(V.scalar_tensor_tensor(base, base, float(SLOT), before, ALU.mult, ALU.subtract))

            def rows_of_tokens():
                chained(V.tensor_tensor(upto, upto, by_expert, ALU.subtract))
                chained(V.tensor_tensor(upto, upto, base.unsqueeze(2).to_broadcast([P, E, NT]), ALU.add))
                chained(V.tensor_tensor(rest, ps[:, 7, 0:NT * E].rearrange("p (t e) -> p t e", t=NT),
                                        upto.rearrange("p e t -> p t e"), ALU.add))
                for k, onehot in enumerate((first, second)):
                    chained(V.tensor_tensor(tmp, rest, onehot, ALU.mult))
                    chained(V.tensor_reduce(rs[:, 4 + k], tmp, AX, ALU.add))
                    V.tensor_copy(rows2[:, :, k], rs[:, 4 + k]).then_inc(s["rows_done"], 1)

            def experts_of_slots():
                chained(V.tensor_tensor(rse, C["slot_no"].unsqueeze(2).to_broadcast([P, NS, E]),
                                        slot_end.unsqueeze(1).to_broadcast([P, NS, E]), ALU.is_ge))
                chained(V.tensor_reduce(slot_expert[:], rse, AX, ALU.add))
                chained(V.tensor_scalar(slot_expert[:], slot_expert[:], float(E - 1), None, ALU.min))
                V.tensor_copy(expert_of[:], slot_expert[:]).then_inc(s["route_done"], 1)

            def tokens_low(m, par):
                dve.wait_ge(s["xt_h"], m + 1)
                wait(dve, s["q_psum"], m - 1)
                V.tensor_tensor(xt[:, par, 1], ps[:, 4, 0:256], xt[:, par, 0].bitcast(F32), ALU.subtract).then_inc(s["xt_l"], 1)

            def keys_and_queries(m, par):
                dve.wait_ge(s["kv_psum"], m + 1)
                wait(dve, s["k_l"], m - 1)
                wait(dve, s["kqt_psum"], m - 1)
                V.tensor_tensor(kq_f[:, par, 0:D], ps[:, 4, 0:D], C["tab_k"], ALU.mult).then_inc(s["k_f"], 1)
                dve.wait_ge(s["q_psum"], m + 1)
                V.tensor_tensor(kq_f[:, par, D:2 * D], ps[:, 5, 0:D], C["tab_q"], ALU.mult).then_inc(s["q_f"], 1)

            def transposed_low(n, par):
                dve.wait_ge(s["kqt_h"], n + 1)
                wait(dve, s["across_done"], n - 1)
                V.tensor_tensor(kq_t[:, par, :, 1], ps[:, 5, :].rearrange("p (w n) -> p w n", w=2),
                                kq_t[:, par, :, 0].bitcast(F32), ALU.subtract).then_inc(s["kqt_l"], 1)

            def values_low(n, par):
                dve.wait_ge(s["v_h"], n + 1)
                V.tensor_tensor(v_r[:, par, :, 1], v_f[:, par].rearrange("p (h d) -> p h d", h=H),
                                v_r[:, par, :, 0].bitcast(F32), ALU.subtract).then_inc(s["v_l"], 1)

            def score_low(i, par, g):
                dve.wait_ge(s["s_h"], NB * i + g + 1)
                wait(dve, s["y_psum"], i - 1)
                V.tensor_tensor(s_r[:, par, 1, g], s_f[:, g], s_r[:, par, 0, g].bitcast(F32), ALU.subtract).then_inc(s["s_l_dve"], 1)

            def masked_scores(i, g):
                dve.wait_ge(s["s_psum"], NB * i + g + 1)
                if g % 2 == 0:
                    wait(dve, s["s_l_pool"], 2 * (i - 1) + g // 2 + 1 if not isinstance(i, int) or i > 0 else 0)
                V.tensor_tensor(s_f[:, g].rearrange("p (h i) -> p h i", h=HB), ps[:, g, :].rearrange("p (h i) -> p h i", h=HB),
                                C["causal"].unsqueeze(1).to_broadcast([P, HB, P]), ALU.mult).then_inc(s["s_f"], 1)

            def new_state(m):
                dve.wait_ge(s["u_psum"], m + 1)
                dve.wait_ge(s["st_f"], m + 1)
                V.tensor_tensor(state_t, ps[:, 6, 256:512].rearrange("p (c i) -> p c i", c=KC), state_f, ALU.add).then_inc(s["st_t"], 1)
                dve.wait_ge(s["st_t"], m + 1)
                wait(dve, s["st_h"], m)
                wait(dve, s["st_l"], m)
                V.scalar_tensor_tensor(state_f, state_t, C["keep"][:, bass.ds(m + 1, 1)], decay, ALU.mult, ALU.mult).then_inc(s["st_f"], 1)

            def output_stats(m):
                dve.wait_ge(s["y_t"], m + 1)
                for c in range(KC):
                    V.bn_stats(y_stats[:, c, bass.ds(m, 1)].rearrange("p a k -> p (a k)"),
                               y_t[:, bass.ds(m, 1), c].rearrange("p a i -> p (a i)")).then_inc(s["y_stats"], 1)

            def output_sum(m, par):
                dve.wait_ge(s["y_psum"], m + 1)
                wait(dve, s["yt_psum"], m - 1)
                V.tensor_reduce(y_f[:, par].rearrange("p (h d) -> p h d", h=H),
                                ps[:, 7, :].rearrange("p (h s d) -> p h d s", h=H, s=2), AX, ALU.add).then_inc(s["y_f"], 1)

            def chunk(i, par):
                if within(i + 1, NT):
                    transposed_low(i + 1, 1 - par)
                if within(i, NT):
                    for g in range(NB):
                        masked_scores(i, g)
                if within(i + 2, NT):
                    tokens_low(i + 2, par)
                if within(i, NT):
                    score_low(i, par, 1)
                if within(i - 1, NT):
                    new_state(i - 1)
                if within(i, NT):
                    score_low(i, par, 3)
                if within(i - 3, NT):
                    output_stats(i - 3)
                if within(i - 1, NT):
                    output_sum(i - 1, 1 - par)
                if within(i + 1, NT):
                    values_low(i + 1, 1 - par)
                if within(i + 2, NT):
                    keys_and_queries(i + 2, par)

            shifted_logits()
            tokens_low(0, 0)
            first_expert()
            second_expert()
            keys_and_queries(0, 0)
            slots_of_experts()
            transposed_low(0, 0)
            gate_values()
            tokens_low(1, 1)
            rows_of_tokens()
            values_low(0, 0)
            keys_and_queries(1, 1)
            experts_of_slots()
            dve.wait_ge(s["ln_xn"], NG)
            V.memset(state_f, 0.0).then_inc(s["st_f"], 1)
            run_steps(dve, 0, NT, 4, 28, chunk)

            def xs_low(sl, par):
                dve.wait_ge(s["xst_h"], sl + 1)
                wait(dve, s["h_psum"], FC // 2 * sl)
                V.tensor_tensor(xs_r[:, 1], ps[:, par, :], xs_r[:, 0].bitcast(F32), ALU.subtract).then_inc(s["xst_l"], 1)

            def ys_gated(sl, par):
                dve.wait_ge(s["ys_psum"], sl + 1)
                dve.wait_ge(s[f"bias_in{par}"], (sl - par) * 16 + 32)
                wait(dve, s["pairs_out"], 32 * sl)
                V.tensor_tensor(ys.rearrange("p (j d) -> p j d", j=SJ), ps[:, 6 + par, :].rearrange("p (j d) -> p j d", j=SJ),
                                b2_slot[:, par].unsqueeze(1).to_broadcast([P, SJ, D]), ALU.add).then_inc(s["ys_sum"], 1)
                dve.wait_ge(s["ys_sum"], sl + 1)
                dve.wait_ge(s["pair_slot"], sl + 1)
                for j in range(SJ):
                    last = V.tensor_scalar(ys[:, j * D:(j + 1) * D], ys[:, j * D:(j + 1) * D], gate_slot[:, par, j:j + 1], None, ALU.mult)
                last.then_inc(s["ys_sb"], 1)

            def pair_copy(sl, par):
                dve.wait_ge(s[f"xs_in{par}"], (sl - par) * 8 + 16)
                wait(dve, s["pairs_out"], 32 * (sl - 1))
                V.tensor_copy(gate_slot[:, par], xs[:, par, :, D + 1])
                V.tensor_copy(pair_slot[:, par], xs[:, par, :, D]).then_inc(s["pair_slot"], 1)

            def w2_low(sl, par):
                dve.wait_ge(s["w2_h"], sl + 1)
                V.tensor_tensor(w2_r[par][:, 1, W2_POOL:FC * D], w2_raw[par][:, W2_POOL:FC * D], w2_r[par][:, 0, W2_POOL:FC * D].bitcast(F32),
                                ALU.subtract).then_inc(s["w2_l_dve"], 1)

            def slot_step(sl, par):
                for hp in range(FC // 2):
                    m = sl * (FC // 2) + hp
                    cols = slice(hp * 2 * SLOT, (hp + 1) * 2 * SLOT)
                    dve.wait_ge(s["h_f"], m + 1)
                    wait(dve, s["ys_psum"], sl)
                    V.tensor_copy(h_r[:, 0, cols], h_f[:, hp % 2]).then_inc(s["h_h"], 1)
                    dve.wait_ge(s["h_h"], m + 1)
                    V.tensor_tensor(h_r[:, 1, cols], h_f[:, hp % 2], h_r[:, 0, cols].bitcast(F32), ALU.subtract).then_inc(s["h_l"], 1)
                    if hp == 1:
                        if within(sl - 1, NS):
                            ys_gated(sl - 1, 1 - par)
                        pair_copy(sl, par)
                if within(sl + 1, NS):
                    xs_low(sl + 1, 1 - par)
                    w2_low(sl + 1, 1 - par)

            w2_low(0, 0)
            xs_low(0, 0)
            chunk(NT, NT % 2)
            chunk(NT + 1, 1 - NT % 2)
            chunk(NT + 2, NT % 2)
            slot_step(0, 0)
            slot_step(1, 1)

            gn_count = [0]

            def gn(ins):
                gn_count[0] += 1
                ins.then_inc(s["gn_chain"], 1)
                dve.wait_ge(s["gn_chain"], gn_count[0])

            dve.wait_ge(s["gn_in"], 16)
            dve.wait_ge(s["y_stats"], KC * NT)
            for b in range(B):
                for c in range(KC):
                    last = V.bn_aggr(y_mv[:, b, c], y_stats[:, c, b * CB:(b + 1) * CB].rearrange("p a b -> p (a b)"))
            gn(last)
            mean, square, head_mean, head_square, var, std_, scale_t, shift_t = (gn_t[:, k] for k in range(8))
            gn(V.tensor_tensor(square, y_mv[:, :, :, 0], y_mv[:, :, :, 0], ALU.mult))
            V.tensor_copy(mean, y_mv[:, :, :, 0]).then_inc(s["gn_chain"], 1)
            V.tensor_tensor(square, square, y_mv[:, :, :, 1], ALU.add).then_inc(s["gn_chain"], 1)
            gn_count[0] += 2
            dve.wait_ge(s["gn_avg_psum"], 1)
            gn(V.tensor_copy(gn_t[:, 2:4].rearrange("p a b c -> p (a b c)"), ps[:, 6, 0:2 * B * KC]))
            gn(V.tensor_tensor(var, head_mean, head_mean, ALU.mult))
            V.tensor_tensor(var, head_square, var, ALU.subtract).then_inc(s["gn_var"], 1)
            dve.wait_ge(s["gn_std"], 1)
            gn(V.reciprocal(std_, std_))
            gn(V.tensor_tensor(scale_t, std_, gn_sb[:, 0].unsqueeze(1).to_broadcast([P, B, KC]), ALU.mult))
            gn(V.tensor_tensor(shift_t, head_mean, scale_t, ALU.mult))
            gn(V.tensor_tensor(shift_t, gn_sb[:, 1].unsqueeze(1).to_broadcast([P, B, KC]), shift_t, ALU.subtract))
            for k, src in enumerate((scale_t, shift_t)):
                V.tensor_copy(gn_ab[:, k], src.unsqueeze(2).to_broadcast([P, B, 2, KC])).then_inc(s["gn_ab"], 1)

            run_steps(dve, 2, NS, 2, NS - 1, slot_step)
            ys_gated(NS - 1, (NS - 1) % 2)

            def low_half(hb, par):
                dve.wait_ge(s["yn_h"], hb + 1)
                wait(dve, s["o_psum"], hb - 1)
                V.tensor_tensor(yn_r[:, par, 1].rearrange("p c (t i) -> p t c i", t=4), y_t[:, hb * 4:hb * 4 + 4],
                                yn_r[:, par, 0].bitcast(F32).rearrange("p c (t i) -> p t c i", t=4), ALU.subtract).then_inc(s["yn_l"], 1)

            def out_half(hb, par):
                if within(hb + 1, 2 * B):
                    low_half(hb + 1, 1 - par)
                half = x_rows(hb * 4, 4).rearrange("p t d -> p (t d)")
                dve.wait_ge(s[f"x_res_in{hb // 2}"], 16)
                dve.wait_ge(s["o_psum"], hb + 1)
                V.tensor_tensor(half, half, ps[:, par * 2:par * 2 + 2, :].rearrange("p a b -> p (a b)"), ALU.add).then_inc(s["attn_res"], 1)
                dve.wait_ge(s["attn_res"], hb + 1)
                for q in (2 * hb, 2 * hb + 1):
                    dve.wait_ge(s["y_sum"], q + 1)
                    V.tensor_tensor(x_rows(q * 2, 2), x_rows(q * 2, 2), y_pair[:, q % 4, :, 0], ALU.add).then_inc(s["out_sb"], 1)

            low_half(0, 0)
            for hb in range(2 * B):
                out_half(hb, hb % 2)


def kernel(L0_attn_x, L0_attn_W_q, L0_attn_W_k, L0_attn_W_v, L0_attn_W_o, L0_attn_gn_weight, L0_attn_gn_bias,
           L0_ffn_gate_w, L0_ffn_gate_b, L0_ffn_w1, L0_ffn_b1, L0_ffn_w2, L0_ffn_b2):
    import concourse.bacc as bacc
    from concourse.bass_utils import run_bass_kernel_spmd

    const, where = constants()
    a = np.asarray
    gn = np.stack([a(L0_attn_gn_weight).reshape(KC, P), a(L0_attn_gn_bias).reshape(KC, P)]).transpose(2, 0, 1)
    arrays = {
        "x": a(L0_attn_x),
        "wq_t": a(L0_attn_W_q).T,
        "wkv_t": np.concatenate([a(L0_attn_W_k).T, a(L0_attn_W_v).T], 1),
        "wo_t": a(L0_attn_W_o).T,
        "gn": gn,
        "gate_t": a(L0_ffn_gate_w).T,
        "gate_b": a(L0_ffn_gate_b),
        "w1": a(L0_ffn_w1).reshape(E, KC, P, F).transpose(0, 2, 1, 3).reshape(E, P, KC * F),
        "w2": a(L0_ffn_w2).reshape(E, FC, P, D).transpose(0, 2, 1, 3).reshape(E, P, FC * D),
        "b1": a(L0_ffn_b1).reshape(E, FC, P).transpose(0, 2, 1),
        "b2": a(L0_ffn_b2),
        "const": const,
    }
    arrays = {k: np.ascontiguousarray(v) for k, v in arrays.items()}
    nc = bacc.Bacc("TRN2", target_bir_lowering=False, num_devices=1)
    args = {k: nc.dram_tensor(k, v.shape, mybir.dt.from_np(v.dtype), kind="ExternalInput").ap() for k, v in arrays.items()}
    out = nc.dram_tensor("out", (B, T, D), F32, kind="ExternalOutput").ap()
    build(nc, where, out=out, **args)
    r = run_bass_kernel_spmd(nc, [arrays], core_ids=[0])
    return r.results[0]["out"]
```
